# Optimizing a Trainium2 kernel written in Bass

```python
import numpy as np
import jax
import jax.numpy as jnp

def _softmax(x, axis=-1):
    return jax.nn.softmax(x, axis=axis)
def _gelu(x):
    return jax.nn.gelu(x, approximate=True)
def _silu(x):
    return jax.nn.silu(x)
def _sigmoid(x):
    return jax.nn.sigmoid(x)
def _layernorm(x, axis=-1, eps=1e-5):
    m = jnp.mean(x, axis=axis, keepdims=True)
    v = jnp.var(x, axis=axis, keepdims=True)
    return (x - m) / jnp.sqrt(v + eps)
def _scatter_add(tgt, idx, src, axis=0):
    return tgt.at[idx].add(src)
def _segment_sum(src, seg, n):
    return jax.ops.segment_sum(src, seg, n)

kernel_name = 'mk_conv_seq_d1_conv_nchw256_136b67'

def setup_inputs(seed: int = 0):
    np.random.seed(seed)
    _w = jnp.asarray
    def _rec_inputs():
        import jax
        import jax.numpy as jnp
        _gk = jax.random.key(seed)
        x = -0.0002928 + 1 * jax.random.normal(jax.random.fold_in(_gk, 1), (4, 256, 64, 64), jnp.float32)
        return x
    x = _rec_inputs()
    def _L0_conv_setup():
        import jax, jax.numpy as jnp
        import numpy as np
        B, C, H, W = (4, 256, 64, 64)
        CK = C // 8
        key = jax.random.key(seed)
        ks = jax.random.split(key, 9)
        s = 0.02
        return {'x': jax.random.normal(ks[0], (B, C, H, W), dtype=jnp.float32), 'Wq': jax.random.normal(ks[1], (CK, C), dtype=jnp.float32) * s, 'bq': jnp.zeros((CK,), dtype=jnp.float32), 'Wk': jax.random.normal(ks[2], (CK, C), dtype=jnp.float32) * s, 'bk': jnp.zeros((CK,), dtype=jnp.float32), 'Wv': jax.random.normal(ks[3], (C, C), dtype=jnp.float32) * s, 'bv': jnp.zeros((C,), dtype=jnp.float32), 'gamma': jnp.asarray(0.01, dtype=jnp.float32), 'Wf': jax.random.normal(ks[4], (C, 2 * C), dtype=jnp.float32) * s, 'bf': jnp.zeros((C,), dtype=jnp.float32)}
    _L0_conv_all = _L0_conv_setup()
    _L0_conv_in = {k: v for k, v in _L0_conv_all.items() if k in ('Wq', 'bq', 'Wk', 'bk', 'Wv', 'bv', 'gamma', 'Wf', 'bf', )}
    del _L0_conv_all

    return {
        "x": x,
        "L0_conv_Wq": _L0_conv_in["Wq"],
        "L0_conv_bq": _L0_conv_in["bq"],
        "L0_conv_Wk": _L0_conv_in["Wk"],
        "L0_conv_bk": _L0_conv_in["bk"],
        "L0_conv_Wv": _L0_conv_in["Wv"],
        "L0_conv_bv": _L0_conv_in["bv"],
        "L0_conv_gamma": _L0_conv_in["gamma"],
        "L0_conv_Wf": _L0_conv_in["Wf"],
        "L0_conv_bf": _L0_conv_in["bf"],
    }

def reference(x, L0_conv_Wq, L0_conv_bq, L0_conv_Wk, L0_conv_bk, L0_conv_Wv, L0_conv_bv, L0_conv_gamma, L0_conv_Wf, L0_conv_bf):
    import jax
    import jax.numpy as jnp
    def _L0_conv_ref(x, Wq, bq, Wk, bk, Wv, bv, gamma, Wf, bf):
        import jax, jax.numpy as jnp
        import numpy as np
        B, C, H, W = (4, 256, 64, 64)
        CK = C // 8
        b, c, h, w = x.shape
        n = h * w
        xf = x.reshape(b, c, n)
        q = jnp.einsum('oc,bcn->bon', Wq, xf) + bq[None, :, None]
        k = jnp.einsum('oc,bcn->bon', Wk, xf) + bk[None, :, None]
        v = jnp.einsum('oc,bcn->bon', Wv, xf) + bv[None, :, None]
        d_k = q.shape[1]
        att = jnp.einsum('bdi,bdj->bij', q, k) / jnp.sqrt(jnp.asarray(d_k, x.dtype))
        att = jax.nn.softmax(att, axis=-1)
        out = jnp.einsum('bcj,bij->bci', v, att).reshape(b, c, h, w)
        out = gamma * out
        cat = jnp.concatenate([out, x], axis=1)
        fused = jnp.einsum('oc,bchw->bohw', Wf, cat) + bf[None, :, None, None]
        return fused

    def _gn(v, G=32, eps=1e-5):
        B_, C_, H_, W_ = v.shape
        g = v.reshape(B_, G, C_ // G, H_, W_)
        m = jnp.mean(g, axis=(2, 3, 4), keepdims=True)
        s = jnp.var(g, axis=(2, 3, 4), keepdims=True)
        return ((g - m) / jnp.sqrt(s + eps)).reshape(v.shape)

    def _ln_c(v, eps=1e-6):
        m = jnp.mean(v, axis=1, keepdims=True)
        s = jnp.var(v, axis=1, keepdims=True)
        return (v - m) / jnp.sqrt(s + eps)

    def _ln_t(v, eps=1e-5):
        m = jnp.mean(v, axis=-1, keepdims=True)
        s = jnp.var(v, axis=-1, keepdims=True)
        return (v - m) / jnp.sqrt(s + eps)

    def _to_tokens(v):
        B_, C_, H_, W_ = v.shape
        return v.reshape(B_, C_, H_ * W_).transpose(0, 2, 1)
    def _from_tokens(t, like):
        B_, C_, H_, W_ = like.shape
        return t.transpose(0, 2, 1).reshape(B_, C_, H_, W_)

    x = _L0_conv_ref(x, L0_conv_Wq, L0_conv_bq, L0_conv_Wk, L0_conv_bk, L0_conv_Wv, L0_conv_bv, L0_conv_gamma, L0_conv_Wf, L0_conv_bf)
    return x


_drawn_inputs = setup_inputs


def setup_inputs(seed=0):
    import zlib

    import numpy as np

    out = dict(_drawn_inputs(seed))
    spreads = {'L0_conv_bq': (0.0, 2.0),
     'L0_conv_bk': (0.0, 2.0),
     'L0_conv_bv': (0.0, 2.0),
     'L0_conv_bf': (0.0, 0.1)}
    factors = {'L0_conv_Wq': 25.934, 'L0_conv_Wk': 25.584, 'L0_conv_Wv': 25.517}
    for name, (base, spread) in spreads.items():
        noise = np.random.default_rng([zlib.crc32(name.encode()), seed]).standard_normal(out[name].shape)
        drawn = base * np.exp(spread * noise) if base else spread * noise
        out[name] = jnp.asarray(drawn.astype(out[name].dtype))
    for name, factor in factors.items():
        out[name] = (out[name] * factor).astype(out[name].dtype)
    return out
```

```python
import concourse.bass as bass
from concourse import mybir
from contextlib import ExitStack

F32 = mybir.dt.float32
F32R = mybir.dt.float32r
ALU = mybir.AluOpType
ACT = mybir.ActivationFunctionType
AX_X = mybir.AxisListType.X

P = 128
W = 512


def attention_conv(nc, x, wqT, bq, wkT, bk, wv, bv, gamma, wf1T, wf2T, bf, out):
    IMAGES, C_IN, N = x.shape
    CK = wqT.shape[1]
    KT = C_IN // P
    CHUNKS = N // W
    JT = N // P
    PAIRS = JT // 2
    QT = W // P
    JC = W // P
    MAXMM = QT * CHUNKS
    R3 = 3 * CK
    RM = R3 + 2
    SCALE = float(CK) ** -0.5
    LAST = CHUNKS - 1
    FIN_SLOT = 11
    assert C_IN == KT * P == 2 * P and R3 == 96 and CHUNKS == 8 and PAIRS == 16

    x_v = x.rearrange("b (k p) n -> b p k n", p=P)
    out_v = out.rearrange("b (k p) n -> b p k n", p=P)

    with ExitStack() as ctx:
        def sb(name, shape, dt):
            return ctx.enter_context(nc.sbuf_tensor(name, shape, dt))

        def sem(name):
            return ctx.enter_context(nc.semaphore(name))

        keys = sb("keys", [RM, N], F32R)
        queries = sb("queries", [RM, N], F32R)
        q_stat = sb("q_stat", [R3, W], F32R)
        val_hi = sb("val_hi", [P, JT, C_IN], F32R)
        val_lo = sb("val_lo", [P, JT, C_IN], F32R)
        conv = sb("conv", [P, KT, N], F32)
        xf = sb("xf", [P, 2, KT, W], F32)
        probs = sb("probs", [P, 2, 2, W], F32)
        hi = sb("hi", [P, 2, 2, W], F32R)
        lo = sb("lo", [P, 2, 2, W], F32R)
        acc = sb("acc", [P, 2, W], F32)
        acc_sum = sb("acc_sum", [P, W], F32)
        acc_hi = sb("acc_hi", [P, W], F32R)
        acc_lo = sb("acc_lo", [P, W], F32R)
        o_raw = sb("o_raw", [P, KT, W], F32)
        part_max = sb("part_max", [P, QT, CHUNKS], F32)
        cols = sb("cols", [P, QT, RM], F32R)
        rows = sb("rows", [RM, W], F32R)
        neg_max = sb("neg_max", [P, QT, 1], F32)
        inv_sum = sb("inv_sum", [P, QT, 1], F32)
        wvf_hi = sb("wvf_hi", [P, KT, C_IN], F32R)
        wvf_lo = sb("wvf_lo", [P, KT, C_IN], F32R)
        wf2_hi = sb("wf2_hi", [P, KT, C_IN], F32R)
        wf2_lo = sb("wf2_lo", [P, KT, C_IN], F32R)
        wq3_hi = sb("wq3_hi", [P, KT, R3], F32R)
        wq3_lo = sb("wq3_lo", [P, KT, R3], F32R)
        wk3_hi = sb("wk3_hi", [P, KT, R3], F32R)
        wk3_lo = sb("wk3_lo", [P, KT, R3], F32R)
        ident = sb("ident", [P, P], F32R)
        pick = sb("pick", [RM, P], F32R)
        ones = sb("ones", [P, 2], F32R)
        bq3 = sb("bq3", [R3, 1], F32)
        bk3 = sb("bk3", [R3, 1], F32)
        bv_c = sb("bv_c", [P, KT], F32)
        bf_c = sb("bf_c", [P, KT], F32)
        bias = sb("bias", [P, KT], F32)
        gam = sb("gam", [P, 1], F32)
        raw = conv[:, 0, :]
        wv_raw = raw[:, 0:512].rearrange("p (k n) -> p k n", k=KT)
        wf1_raw = raw[:, 512:1024].rearrange("p (k n) -> p k n", k=KT)
        wf2_raw = raw[:, 1024:1536].rearrange("p (k n) -> p k n", k=KT)
        wq_raw = raw[:, 1536:1536 + KT * CK].rearrange("p (k n) -> p k n", k=KT)
        wk_raw = raw[:, 1664:1664 + KT * CK].rearrange("p (k n) -> p k n", k=KT)
        id_raw = raw[:, 1792:1920]

        ps_s = ctx.enter_context(nc.psum_tensor("ps_s", [P, 4, W], F32))
        ps_m = ctx.enter_context(nc.psum_tensor("ps_m", [P, 2, W], F32))
        ps_o = ctx.enter_context(nc.psum_tensor("ps_o", [P, KT, W], F32))

        w_loaded = sem("w_loaded")
        id_zeroed = sem("id_zeroed")
        pick_zeroed = sem("pick_zeroed")
        id_made = sem("id_made")
        w_hi_done = sem("w_hi_done")
        w_split = sem("w_split")
        wvf_ready = sem("wvf_ready")
        wvf_hi_done = sem("wvf_hi_done")
        consts_done = sem("consts_done")
        x_loaded = [sem(f"x_loaded{i}") for i in range(2)]
        x_hi_done = sem("x_hi_done")
        x_split = sem("x_split")
        k_ready, k_hi_done, k_split = sem("k_ready"), sem("k_hi_done"), sem("k_split")
        q_ready, q_hi_done, q_split = sem("q_ready"), sem("q_hi_done"), sem("q_split")
        conv_ready, conv_done = sem("conv_ready"), sem("conv_done")
        v_ready, v_hi_done, v_free = sem("v_ready"), sem("v_hi_done"), sem("v_free")
        q_stat_ready = sem("q_stat_ready")
        m_ready, m_free = sem("m_ready"), sem("m_free")
        neg_max_done, cols_hi_done, cols_ready = sem("neg_max_done"), sem("cols_hi_done"), sem("cols_ready")
        rows_ready, rows_copied, max_rows_copied = sem("rows_ready"), sem("rows_copied"), sem("max_rows_copied")
        s_ready, exp_done = sem("s_ready"), sem("exp_done")
        p_hi_done, p_lo_done, pv_done = sem("p_hi_done"), sem("p_lo_done"), sem("pv_done")
        acc_done, acc_folded = sem("acc_done"), sem("acc_folded")
        acc_hi_done, acc_lo_done = sem("acc_hi_done"), sem("acc_lo_done")
        sums_ready, inv_done, inv_hi_done, inv_cols = sem("sums_ready"), sem("inv_done"), sem("inv_hi_done"), sem("inv_cols")
        o_copied0, o_copied1, o_raw_free = sem("o_copied0"), sem("o_copied1"), sem("o_raw_free")
        factor_ready, o_scaled, finished = sem("factor_ready"), sem("o_scaled"), sem("finished")
        stored = [sem(f"stored{i}") for i in range(CHUNKS)]

        def span(n):
            return bass.ds(n * W, W)

        block = ctx.enter_context(nc.Block())

        @block.sync
        def _(sp):
            NW = 0
            for dst, src in (
                (wv_raw, wv.rearrange("(k p) n -> p k n", p=P)),
                (wf1_raw, wf1T.rearrange("(k p) n -> p k n", p=P)),
                (wf2_raw, wf2T.rearrange("(k p) n -> p k n", p=P)),
                (wq_raw, wqT.rearrange("(k p) n -> p k n", p=P)),
                (wk_raw, wkT.rearrange("(k p) n -> p k n", p=P)),
                (bv_c[:], bv),
                (bf_c[:], bf),
                (gam[:], gamma.broadcast_to((P, 1))),
                (bq3[0:CK], bq), (bq3[CK:2 * CK], bq), (bq3[2 * CK:R3], bq),
                (bk3[0:CK], bk), (bk3[CK:2 * CK], bk), (bk3[2 * CK:R3], bk),
            ):
                sp.dma_start(dst, src).then_inc(w_loaded, 16)
                NW += 1
            assert NW == N_WEIGHT_LOADS

            def load(b, c):
                sp.dma_start(xf[:, c % 2], x_v[bass.ds(b, 1), :, :, c * W:(c + 1) * W].rearrange(
                    "b p k n -> p (b k) n")).then_inc(x_loaded[c % 2], 16)

            def store(b, n):
                sp.wait_ge(finished, b * CHUNKS + (n + 2))
                sp.dma_start(out_v[bass.ds(b, 1), :, :, n * W:(n + 1) * W].rearrange("b p k n -> p (b k) n"),
                             conv[:, :, n * W:(n + 1) * W]).then_inc(stored[n], 16)

            for c in range(CHUNKS):
                if c >= 2:
                    sp.wait_ge(x_split, c - 1)
                load(0, c)
            with sp.Fori(0, IMAGES - 1) as b:
                for n in range(LAST):
                    store(b, n)
                for c in range(CHUNKS):
                    if c == 2:
                        store(b, LAST)
                    sp.wait_ge(x_split, b * CHUNKS + (CHUNKS + c - 1))
                    sp.wait_ge(stored[c], b * 16 + 16)
                    load(b + 1, c)
            for n in range(CHUNKS):
                store(IMAGES - 1, n)
            for n in range(CHUNKS):
                sp.wait_ge(stored[n], 16 * IMAGES)

        @block.tensor
        def _(pe):
            pe.wait_ge(w_loaded, 16 * N_WEIGHT_LOADS)
            for ct in range(KT):
                for k in range(KT):
                    nc.tensor.matmul(ps_o[:, ct, 0:C_IN], wv_raw[:, k, ct * P:(ct + 1) * P], wf1_raw[:, k, :],
                                     start=(k == 0), stop=(k == KT - 1))
            for ot in range(KT):
                for k in range(KT):
                    last = nc.tensor.matmul(ps_m[:, ot, 0:1], wf1_raw[:, k, ot * P:(ot + 1) * P], bv_c[:, k:k + 1],
                                            start=(k == 0), stop=(k == KT - 1))
            last.then_inc(wvf_ready, 1)
            pe.wait_ge(w_split, 1)

            def product3(dst, a_hi, a_lo, b_hi, b_lo):
                terms = [(a, b, k) for k in range(KT) for a, b in ((a_hi, b_hi), (a_hi, b_lo), (a_lo, b_hi))]
                for i, (a, b, k) in enumerate(terms):
                    last = nc.tensor.matmul(dst, a(k), b(k), start=(i == 0), stop=(i == len(terms) - 1))
                return last

            def max_scores(B, k):
                i, c = k % QT, k // QT
                pe.wait_ge(m_free, B * MAXMM + k + 1)
                nc.tensor.matmul(ps_m[:, k % 2], q_stat[:, i * P:(i + 1) * P], keys[0:R3, c * W:(c + 1) * W],
                                 start=True, stop=True).then_inc(m_ready, 1)

            def project(b, c2, p):
                c = c2 * 2 + p
                C = pe.snap(b * CHUNKS + c)
                xh = lambda k: hi[:, p, k, :]
                xl = lambda k: lo[:, p, k, :]
                pe.wait_ge(x_split, C + 1)
                product3(ps_s[0:R3, 0], lambda k: wk3_hi[:, k], lambda k: wk3_lo[:, k], xh, xl).then_inc(k_ready, 1)
                product3(ps_s[0:R3, 1], lambda k: wq3_hi[:, k], lambda k: wq3_lo[:, k], xh, xl).then_inc(q_ready, 1)
                for ot in range(KT):
                    product3(ps_s[:, 2 + ot], lambda k: wf2_hi[:, k, ot * P:(ot + 1) * P],
                             lambda k: wf2_lo[:, k, ot * P:(ot + 1) * P], xh, xl).then_inc(conv_ready, 1)
                for j in range(JC):
                    if j % 2 == 0:
                        pe.wait_ge(v_free, C * 2 + (j // 2 + 1))
                    last = product3(ps_o[:, j // 2, (j % 2) * C_IN:(j % 2 + 1) * C_IN],
                                    lambda k: hi[:, p, k, j * P:(j + 1) * P],
                                    lambda k: lo[:, p, k, j * P:(j + 1) * P],
                                    lambda k: wvf_hi[:, k], lambda k: wvf_lo[:, k])
                    if j % 2:
                        last.then_inc(v_ready, 1)
                    if j == 0:
                        pe.wait_ge(k_split, C + 1)
                        pe.wait_ge(q_stat_ready, b * CHUNKS + 1)
                    if j == JC - 1:
                        pe.wait_ge(q_split, C + 1)
                        pe.wait_ge(conv_done, C * 2 + 2)
                    pe.wait_ge(m_free, b * (CHUNKS * MAXMM) + (c * QT + (j + 1)))
                    nc.tensor.matmul(ps_m[:, j % 2], q_stat[:, j * P:(j + 1) * P], keys[0:R3, span(c)],
                                     start=True, stop=True).then_inc(m_ready, 1)

            def turn_columns(B):
                pe.wait_ge(cols_ready, B)
                for i in range(QT):
                    last = nc.tensor.matmul(ps_m[0:RM, 0, i * P:(i + 1) * P], cols[:, i, :], ident[:],
                                            start=True, stop=True)
                last.then_inc(rows_ready, 1)

            def sum_probs(B):
                pe.wait_ge(acc_lo_done, B)
                for i in range(QT):
                    nc.tensor.matmul(ps_m[:, 1, 2 * i:2 * i + 2], acc_hi[:, i * P:(i + 1) * P], ones[:],
                                     start=True, stop=False)
                    last = nc.tensor.matmul(ps_m[:, 1, 2 * i:2 * i + 2], acc_lo[:, i * P:(i + 1) * P], ones[:],
                                            start=False, stop=True)
                last.then_inc(sums_ready, 1)

            def spread_factor(turns):
                pe.wait_ge(rows_copied, turns)
                nc.tensor.matmul(ps_m[:, 1], pick[:], rows[:], start=True, stop=True).then_inc(factor_ready, 1)

            def scores(n, t):
                for h in range(2):
                    j = 2 * t + h
                    last = nc.tensor.matmul(ps_s[:, 2 * (t % 2) + h], keys[:, j * P:(j + 1) * P], queries[:, span(n)],
                                            start=True, stop=True)
                last.then_inc(s_ready, 1)

            def attend(b, n, first, last_block):
                B = pe.snap(b * CHUNKS + n)
                for t in range(PAIRS):
                    if t < PAIRS - 2:
                        pe.wait_ge(exp_done, B * PAIRS + (t + 1))
                        scores(n, t + 2)
                    elif not last_block:
                        if t == PAIRS - 2:
                            pe.wait_ge(max_rows_copied, B + 2)
                        pe.wait_ge(exp_done, B * PAIRS + (t + 1))
                        scores(n + 1, t + 2 - PAIRS)
                    if not first and t == FIN_SLOT:
                        if not last_block:
                            pe.wait_ge(m_free, B * MAXMM + (2 * MAXMM + 2))
                        sum_probs(B)
                    if t == FIN_SLOT + 1:
                        turn_columns(b * (CHUNKS + 2) + (n + 2))
                    if not first and t == FIN_SLOT + 2:
                        spread_factor(B)
                    if not first and t == FIN_SLOT + 3:
                        pe.wait_ge(o_scaled, B)
                    terms = [(v, hi, h, c) for h in range(2) for c in range(KT) for v in (val_hi, val_lo)]
                    terms += [(val_hi, lo, h, c) for h in range(2) for c in range(KT)]
                    pe.wait_ge(p_hi_done, B * PAIRS + (t + 1))
                    if t == 0 and first:
                        pe.wait_ge(v_free, b * (2 * CHUNKS) + (2 * CHUNKS + 2))
                    elif t == 0:
                        pe.wait_ge(o_copied0, B)
                        pe.wait_ge(o_copied1, B)
                    for i, (v, p, h, c) in enumerate(terms):
                        if i == 8:
                            pe.wait_ge(p_lo_done, B * PAIRS + (t + 1))
                        last = nc.tensor.matmul(ps_o[:, c], v[:, 2 * t + h, c * P:(c + 1) * P], p[:, t % 2, h, :],
                                                start=(t == 0 and i in (0, 2)),
                                                stop=(t == PAIRS - 1 and i >= len(terms) - 2))
                        if i == len(terms) - 1:
                            last.then_inc(pv_done, 1)
                        k = 3 * t + i // 4
                        if not last_block and i % 4 == 1 and k < MAXMM:
                            if k == 0:
                                pe.wait_ge(q_stat_ready, B + 2)
                            max_scores(B + 1, k)

            with pe.Fori(0, IMAGES) as b:
                project(b, 0, 0)
                project(b, 0, 1)
                with pe.Fori(1, CHUNKS // 2) as c2:
                    project(b, c2, 0)
                    project(b, c2, 1)
                turn_columns(b * (CHUNKS + 2) + 1)
                pe.wait_ge(max_rows_copied, b * CHUNKS + 1)
                scores(0, 0)
                scores(0, 1)
                attend(b, 0, True, False)
                with pe.Fori(1, LAST) as n:
                    attend(b, n, False, False)
                attend(b, LAST, False, True)
                B = pe.snap(b * CHUNKS + CHUNKS)
                sum_probs(B)
                turn_columns(b * (CHUNKS + 2) + (CHUNKS + 2))
                spread_factor(B)
                pe.wait_ge(o_scaled, B)
                pe.wait_ge(o_copied0, B)
                pe.wait_ge(o_copied1, B)

        @block.scalar
        def _(act):
            act.wait_ge(w_loaded, 16 * N_WEIGHT_LOADS)
            for r in range(3):
                nc.scalar.activation(wk3_hi[:, :, r * CK:(r + 1) * CK], wk_raw, ACT.Copy)
                nc.scalar.activation(wq3_hi[:, :, r * CK:(r + 1) * CK], wq_raw, ACT.Copy)
            nc.scalar.activation(wf2_hi[:], wf2_raw, ACT.Copy).then_inc(w_hi_done, 1)
            act.wait_ge(wvf_ready, 1)
            nc.scalar.activation(wvf_hi[:], ps_o[:, :, 0:C_IN], ACT.Copy).then_inc(wvf_hi_done, 1)
            act.wait_ge(w_split, 1)

            def split_x(C, p, k, reused):
                act.wait_ge(x_loaded[p], k * 16)
                if reused:
                    act.wait_ge(v_ready, C * 2 - 2)
                nc.scalar.activation(hi[:, p], xf[:, p], ACT.Copy).then_inc(x_hi_done, 1)

            def project(b, c2, p, ahead):
                c = c2 * 2 + p
                C = act.snap(b * CHUNKS + c)
                act.wait_ge(k_ready, C + 1)
                nc.scalar.activation(keys[0:R3, span(c)], ps_s[0:R3, 0], ACT.Identity, bias=bk3[:, 0:1]).then_inc(k_hi_done, 1)
                act.wait_ge(q_ready, C + 1)
                nc.scalar.activation(queries[0:R3, span(c)], ps_s[0:R3, 1], ACT.Identity, bias=bq3[:, 0:1]).then_inc(q_hi_done, 1)
                if ahead:
                    split_x(C + 1, 1 - p, b * (CHUNKS // 2) + (c2 + p) + 1, not (isinstance(c, int) and c == 0))
                for ot in range(KT):
                    act.wait_ge(conv_ready, C * 2 + (ot + 1))
                    nc.scalar.activation(conv[:, ot, span(c)], ps_s[:, 2 + ot], ACT.Identity,
                                         bias=bias[:, ot:ot + 1]).then_inc(conv_done, 1)
                for h in range(2):
                    act.wait_ge(v_ready, C * 2 + (h + 1))
                    nc.scalar.activation(val_hi[:, bass.ds(c * JC + 2 * h, 2), :],
                                         ps_o[:, h].rearrange("p (j c) -> p j c", j=2), ACT.Copy).then_inc(v_hi_done, 1)

            def exp(B, t):
                act.wait_ge(s_ready, B * PAIRS + (t + 1))
                nc.scalar.activation(probs[:, t % 2], ps_s[:, 2 * (t % 2):2 * (t % 2) + 2], ACT.Exp,
                                     scale=SCALE).then_inc(exp_done, 1)

            def split_p(B, t):
                act.wait_ge(exp_done, B * PAIRS + (t + 1))
                nc.scalar.activation(hi[:, t % 2], probs[:, t % 2], ACT.Copy).then_inc(p_hi_done, 1)

            def copy_sums(B):
                act.wait_ge(pv_done, B * PAIRS)
                act.wait_ge(finished, B)
                nc.scalar.activation(o_raw[:, 0], ps_o[:, 0], ACT.Copy).then_inc(o_copied0, 1)

            def attend(b, n, first, last_block):
                B = act.snap(b * CHUNKS + n)
                for t in range(PAIRS):
                    if t == 0 and not first:
                        copy_sums(B)
                    if t < PAIRS - 2 or not last_block:
                        act.wait_ge(acc_done, B * (PAIRS - 1) + max(t, 1))
                        act.wait_ge(p_lo_done, B * PAIRS + (t + 1))
                        exp(B, t + 2)
                    if t < PAIRS - 1 or not last_block:
                        if t > 0 or not first:
                            act.wait_ge(pv_done, B * PAIRS + t)
                        split_p(B, t + 1)
                act.wait_ge(acc_folded, B + 1)
                nc.scalar.activation(acc_hi[:], acc_sum[:], ACT.Copy).then_inc(acc_hi_done, 1)

            with act.Fori(0, IMAGES) as b:
                split_x(act.snap(b * CHUNKS), 0, b * (CHUNKS // 2) + 1, False)
                project(b, 0, 0, True)
                project(b, 0, 1, True)
                with act.Fori(1, CHUNKS // 2 - 1) as c2:
                    project(b, c2, 0, True)
                    project(b, c2, 1, True)
                project(b, CHUNKS // 2 - 1, 0, True)
                project(b, CHUNKS // 2 - 1, 1, False)
                B = act.snap(b * CHUNKS)
                exp(B, 0)
                exp(B, 1)
                split_p(B, 0)
                attend(b, 0, True, False)
                with act.Fori(1, LAST) as n:
                    attend(b, n, False, False)
                attend(b, LAST, False, True)
                copy_sums(act.snap(b * CHUNKS + CHUNKS))

        @block.vector
        def _(dve):
            nc.vector.memset(ones[:].bitcast(F32), 1.0)
            nc.vector.memset(cols[:].bitcast(F32), 0.0)
            nc.vector.memset(keys[R3:RM, :].bitcast(F32), 1.0)
            nc.vector.memset(pick[:].bitcast(F32), 0.0).then_inc(pick_zeroed, 1)
            dve.wait_ge(pick_zeroed, 1)
            nc.vector.memset(pick[0:2].bitcast(F32), 1.0)
            dve.wait_ge(id_made, 1)
            nc.vector.tensor_copy(ident[:], id_raw)
            dve.wait_ge(w_hi_done, 1)
            for r in range(3):
                s = slice(r * CK, (r + 1) * CK)
                nc.vector.tensor_tensor(wk3_lo[:, :, s], wk_raw, wk3_hi[:, :, s].bitcast(F32), ALU.subtract)
                nc.vector.tensor_tensor(wq3_lo[:, :, s], wq_raw, wq3_hi[:, :, s].bitcast(F32), ALU.subtract)
            nc.vector.tensor_tensor(wf2_lo[:], wf2_raw, wf2_hi[:].bitcast(F32), ALU.subtract)
            dve.wait_ge(wvf_hi_done, 1)
            nc.vector.tensor_tensor(wvf_lo[:], ps_o[:, :, 0:C_IN], wvf_hi[:].bitcast(F32), ALU.subtract)
            nc.vector.scalar_tensor_tensor(bias[:], ps_m[:, :, 0], gam[:, 0:1], bf_c[:], ALU.mult, ALU.add).then_inc(w_split, 1)
            dve.sem_inc(v_free, 2)
            dve.sem_inc(m_free, 2)

            def split_x(C, p):
                dve.wait_ge(x_hi_done, C + 1)
                nc.vector.tensor_tensor(lo[:, p], xf[:, p], hi[:, p].bitcast(F32), ALU.subtract).then_inc(x_split, 1)

            def chunk_max(B, i, c):
                dve.wait_ge(m_ready, B * MAXMM + (c * QT + (i + 1)))
                nc.vector.reduce_max(part_max[:, i, bass.ds(c, 1)], ps_m[:, i % 2], AX_X).then_inc(m_free, 1)

            def project(b, c2, p, ahead):
                c = c2 * 2 + p
                C = dve.snap(b * CHUNKS + c)
                dve.wait_ge(k_hi_done, C + 1)
                klo = keys[2 * CK:R3, span(c)]
                nc.vector.scalar_tensor_tensor(klo, ps_s[2 * CK:R3, 0], bk3[2 * CK:R3, 0:1], klo.bitcast(F32),
                                               ALU.add, ALU.subtract).then_inc(k_split, 1)
                dve.wait_ge(q_hi_done, C + 1)
                qlo = queries[CK:2 * CK, span(c)]
                nc.vector.scalar_tensor_tensor(qlo, ps_s[CK:2 * CK, 1], bq3[CK:2 * CK, 0:1], qlo.bitcast(F32),
                                               ALU.add, ALU.subtract).then_inc(q_split, 1)
                if isinstance(c, int) and c == 0:
                    dve.wait_ge(q_split, C + 1)
                    nc.vector.tensor_copy(q_stat[:], queries[0:R3, 0:W].bitcast(F32)).then_inc(q_stat_ready, 1)
                if ahead:
                    split_x(C + 1, 1 - p)
                for h in range(2):
                    if h == 1:
                        chunk_max(B0(b), 1, c)
                    else:
                        chunk_max(B0(b), 0, c)
                        dve.wait_ge(v_hi_done, C * 2 + 1)
                        split_v(c, 0)
                chunk_max(B0(b), 2, c)
                chunk_max(B0(b), 3, c)
                dve.wait_ge(v_hi_done, C * 2 + 2)
                split_v(c, 1)

            def B0(b):
                return b * CHUNKS

            def split_v(c, h):
                j2 = bass.ds(c * JC + 2 * h, 2)
                nc.vector.tensor_tensor(val_lo[:, j2, :], ps_o[:, h].rearrange("p (j c) -> p j c", j=2),
                                        val_hi[:, j2, :].bitcast(F32), ALU.subtract).then_inc(v_free, 1)

            def split_p(B, t):
                dve.wait_ge(p_hi_done, B * PAIRS + (t + 1))
                nc.vector.tensor_tensor(lo[:, t % 2], probs[:, t % 2], hi[:, t % 2].bitcast(F32),
                                        ALU.subtract).then_inc(p_lo_done, 1)

            def max_columns(B, turn):
                dve.wait_ge(m_free, B * MAXMM + (MAXMM + 2))
                nc.vector.tensor_reduce(neg_max[:], part_max[:], AX_X, ALU.max, negate=True).then_inc(neg_max_done, 1)
                dve.wait_ge(neg_max_done, B + 1)
                nc.vector.tensor_copy(cols[:, :, R3:R3 + 1], neg_max[:]).then_inc(cols_hi_done, 1)
                dve.wait_ge(cols_hi_done, B + 1)
                last = nc.vector.tensor_tensor(cols[:, :, R3 + 1:R3 + 2], neg_max[:],
                                               cols[:, :, R3:R3 + 1].bitcast(F32), ALU.subtract)
                if turn:
                    last.then_inc(cols_ready, 1)

            def inv_columns(B):
                dve.wait_ge(sums_ready, B)
                nc.vector.reciprocal(inv_sum[:], ps_m[:, 1, 0:2 * QT].rearrange("p (q o) -> p q o", o=2)[:, :, 0:1]).then_inc(inv_done, 1)
                dve.wait_ge(inv_done, B)
                nc.vector.tensor_copy(cols[:, :, 0:1], inv_sum[:]).then_inc(inv_hi_done, 1)
                dve.wait_ge(inv_hi_done, B)
                nc.vector.tensor_tensor(cols[:, :, 1:2], inv_sum[:], cols[:, :, 0:1].bitcast(F32),
                                        ALU.subtract).then_inc(cols_ready, 1)

            def copy_max_rows(n):
                nc.vector.tensor_copy(queries[R3:RM, span(n)], ps_m[R3:RM, 0]).then_inc(max_rows_copied, 1)

            def copy_rows():
                nc.vector.tensor_copy(rows[:], ps_m[0:RM, 0]).then_inc(rows_copied, 1)

            def scale_sums(B):
                dve.wait_ge(o_copied0, B)
                dve.wait_ge(o_copied1, B)
                dve.wait_ge(factor_ready, B)
                nc.vector.scalar_tensor_tensor(o_raw[:], o_raw[:], gam[:, 0:1],
                                               ps_m[:, 1:2, :].broadcast_to((P, KT, W)),
                                               ALU.mult, ALU.mult).then_inc(o_scaled, 1)

            def copy_sums(B):
                dve.wait_ge(pv_done, B * PAIRS)
                dve.wait_ge(finished, B)
                nc.vector.tensor_copy(o_raw[:, 1], ps_o[:, 1]).then_inc(o_copied1, 1)

            def attend(b, n, first, last_block):
                B = dve.snap(b * CHUNKS + n)
                for t in range(PAIRS):
                    if t == 0 and not last_block:
                        nc.vector.tensor_copy(q_stat[:], queries[0:R3, span(n + 1)].bitcast(F32)).then_inc(q_stat_ready, 1)
                    if t == 0 and not first:
                        copy_sums(B)
                    ks = [k for k in (3 * t, 3 * t + 1, 3 * t + 2) if k < MAXMM and not last_block]
                    for k in ks[:2]:
                        chunk_max(B + 1, k % QT, k // QT)
                    if t < PAIRS - 1 or not last_block:
                        split_p(B, t + 1)
                    for k in ks[2:]:
                        chunk_max(B + 1, k % QT, k // QT)
                    if t == FIN_SLOT:
                        if not last_block:
                            max_columns(B + 1, first)
                        if not first:
                            inv_columns(B)
                    if t == FIN_SLOT + 1:
                        dve.wait_ge(rows_ready, b * (CHUNKS + 2) + (n + 2))
                        if not last_block:
                            copy_max_rows(n + 1)
                        if not first:
                            copy_rows()
                    if t == FIN_SLOT + 2 and not first:
                        scale_sums(B)
                dve.wait_ge(acc_hi_done, B + 1)
                nc.vector.tensor_tensor(acc_lo[:], acc_sum[:], acc_hi[:].bitcast(F32), ALU.subtract).then_inc(acc_lo_done, 1)

            with dve.Fori(0, IMAGES) as b:
                split_x(dve.snap(b * CHUNKS), 0)
                project(b, 0, 0, True)
                project(b, 0, 1, True)
                with dve.Fori(1, CHUNKS // 2 - 1) as c2:
                    project(b, c2, 0, True)
                    project(b, c2, 1, True)
                project(b, CHUNKS // 2 - 1, 0, True)
                project(b, CHUNKS // 2 - 1, 1, False)
                B = dve.snap(b * CHUNKS)
                max_columns(B, True)
                dve.wait_ge(rows_ready, b * (CHUNKS + 2) + 1)
                copy_max_rows(0)
                split_p(B, 0)
                attend(b, 0, True, False)
                with dve.Fori(1, LAST) as n:
                    attend(b, n, False, False)
                attend(b, LAST, False, True)
                B = dve.snap(b * CHUNKS + CHUNKS)
                copy_sums(B)
                inv_columns(B)
                dve.wait_ge(rows_ready, b * (CHUNKS + 2) + (CHUNKS + 2))
                copy_rows()
                scale_sums(B)

        @block.gpsimd
        def _(pool):
            nc.gpsimd.memset(id_raw, 0.0).then_inc(id_zeroed, 1)
            pool.wait_ge(id_zeroed, 1)
            nc.gpsimd.affine_select(out=id_raw, in_=id_raw, compare_op=ALU.not_equal, fill=1.0, base=0,
                                    pattern=[[-1, P]], channel_multiplier=1).then_inc(id_made, 1)
            pool.sem_inc(finished, 1)

            def add(B, t):
                pool.wait_ge(exp_done, B * PAIRS + (t + 1))
                if t == 1:
                    nc.gpsimd.tensor_tensor(acc[:], probs[:, 0], probs[:, 1], ALU.add).then_inc(acc_done, 1)
                else:
                    pool.wait_ge(acc_done, B * (PAIRS - 1) + (t - 1))
                    nc.gpsimd.tensor_tensor(acc[:], acc[:], probs[:, t % 2], ALU.add).then_inc(acc_done, 1)

            def finish(B, n):
                pool.wait_ge(o_scaled, B)
                nc.gpsimd.tensor_tensor(conv[:, :, span(n)], conv[:, :, span(n)], o_raw[:], ALU.add).then_inc(finished, 1)

            def attend(b, n, first, last_block):
                B = pool.snap(b * CHUNKS + n)
                for t in range(PAIRS):
                    if t == PAIRS - 2:
                        pool.wait_ge(acc_done, B * (PAIRS - 1) + (PAIRS - 1))
                        nc.gpsimd.tensor_tensor(acc_sum[:], acc[:, 0], acc[:, 1], ALU.add).then_inc(acc_folded, 1)
                    if t < PAIRS - 2:
                        add(B, t + 2)
                    elif not last_block and t == PAIRS - 1:
                        pool.wait_ge(acc_folded, B + 1)
                        add(B + 1, 1)
                    if t == FIN_SLOT + 3 and not first:
                        finish(B, n - 1)

            with pool.Fori(0, IMAGES) as b:
                add(pool.snap(b * CHUNKS), 1)
                attend(b, 0, True, False)
                with pool.Fori(1, LAST) as n:
                    attend(b, n, False, False)
                attend(b, LAST, False, True)
                finish(pool.snap(b * CHUNKS + CHUNKS), LAST)


N_WEIGHT_LOADS = 14


def kernel(**inputs):
    import numpy as np
    import concourse.bacc as bacc
    from concourse.bass_utils import run_bass_kernel_spmd

    x = np.asarray(inputs["x"])
    images, c, h, w = x.shape
    wf = np.asarray(inputs["L0_conv_Wf"])
    arrays = {
        "x": x.reshape(images, c, h * w),
        "wqT": np.asarray(inputs["L0_conv_Wq"]).T, "bq": np.asarray(inputs["L0_conv_bq"]).reshape(-1, 1),
        "wkT": np.asarray(inputs["L0_conv_Wk"]).T, "bk": np.asarray(inputs["L0_conv_bk"]).reshape(-1, 1),
        "wv": np.asarray(inputs["L0_conv_Wv"]), "bv": np.asarray(inputs["L0_conv_bv"]).reshape(-1, P).T,
        "gamma": np.asarray(inputs["L0_conv_gamma"]).reshape(1, 1),
        "wf1T": wf[:, :c].T, "wf2T": wf[:, c:].T, "bf": np.asarray(inputs["L0_conv_bf"]).reshape(-1, P).T,
    }
    arrays = {name: np.ascontiguousarray(a) for name, a in arrays.items()}
    nc = bacc.Bacc("TRN2", target_bir_lowering=False, num_devices=1)
    args = [nc.dram_tensor(name, a.shape, mybir.dt.from_np(a.dtype), kind="ExternalInput").ap()
            for name, a in arrays.items()]
    out = nc.dram_tensor("out", (images, c, h * w), F32, kind="ExternalOutput").ap()
    attention_conv(nc, *args, out)
    result = run_bass_kernel_spmd(nc, [arrays], core_ids=[0])
    return result.results[0]["out"].reshape(images, c, h, w)
```

```python
import concourse.bass as bass
from concourse import mybir
from contextlib import ExitStack

F32 = mybir.dt.float32
F32R = mybir.dt.float32r
ALU = mybir.AluOpType
ACT = mybir.ActivationFunctionType
AX_X = mybir.AxisListType.X

P = 128
W = 512


def attention_conv(nc, x, wqT, bq, wkT, bk, wv, bv, gamma, wf1T, wf2T, bf, out):
    IMAGES, C_IN, N = x.shape
    CK = wqT.shape[1]
    KT = C_IN // P
    CHUNKS = N // W
    JT = N // P
    PAIRS = JT // 2
    QT = W // P
    JC = W // P
    MAXMM = QT * CHUNKS
    R3 = 3 * CK
    RM = R3 + 2
    SCALE = float(CK) ** -0.5
    LAST = CHUNKS - 1
    PB = 4
    FIN_SLOT = 11
    assert C_IN == KT * P == 2 * P and R3 == 96 and CHUNKS == 8 and PAIRS == 16

    x_v = x.rearrange("b (k p) n -> b p k n", p=P)
    out_v = out.rearrange("b (k p) n -> b p k n", p=P)

    with ExitStack() as ctx:
        def sb(name, shape, dt):
            return ctx.enter_context(nc.sbuf_tensor(name, shape, dt))

        def sem(name):
            return ctx.enter_context(nc.semaphore(name))

        keys = sb("keys", [RM, N], F32R)
        queries = sb("queries", [RM, N], F32R)
        q_stat = sb("q_stat", [R3, W], F32R)
        val_hi = sb("val_hi", [P, JT, C_IN], F32R)
        val_lo = sb("val_lo", [P, JT, C_IN], F32R)
        conv = sb("conv", [P, KT, N], F32)
        xf = sb("xf", [P, 2, KT, W], F32)
        probs = sb("probs", [P, PB, 2, W], F32)
        hi = sb("hi", [P, 2, 2, W], F32R)
        lo = sb("lo", [P, 2, 2, W], F32R)
        acc = sb("acc", [P, 2, W], F32)
        acc_sum = sb("acc_sum", [P, W], F32)
        acc_hi = sb("acc_hi", [P, W], F32R)
        acc_lo = sb("acc_lo", [P, W], F32R)
        o_raw = sb("o_raw", [P, KT, W], F32)
        part_max = sb("part_max", [P, QT, CHUNKS], F32)
        cols = sb("cols", [P, QT, RM], F32R)
        rows = sb("rows", [RM, W], F32R)
        neg_max = sb("neg_max", [P, QT, 1], F32)
        inv_sum = sb("inv_sum", [P, QT, 1], F32)
        wvf_hi = sb("wvf_hi", [P, KT, C_IN], F32R)
        wvf_lo = sb("wvf_lo", [P, KT, C_IN], F32R)
        wf2_hi = sb("wf2_hi", [P, KT, C_IN], F32R)
        wf2_lo = sb("wf2_lo", [P, KT, C_IN], F32R)
        wq3_hi = sb("wq3_hi", [P, KT, R3], F32R)
        wq3_lo = sb("wq3_lo", [P, KT, R3], F32R)
        wk3_hi = sb("wk3_hi", [P, KT, R3], F32R)
        wk3_lo = sb("wk3_lo", [P, KT, R3], F32R)
        ident = sb("ident", [P, P], F32R)
        pick = sb("pick", [RM, P], F32R)
        ones = sb("ones", [P, 2], F32R)
        bq3 = sb("bq3", [R3, 1], F32)
        bk3 = sb("bk3", [R3, 1], F32)
        bv_c = sb("bv_c", [P, KT], F32)
        bf_c = sb("bf_c", [P, KT], F32)
        bias = sb("bias", [P, KT], F32)
        gam = sb("gam", [P, 1], F32)
        raw = conv[:, 0, :]
        wv_raw = raw[:, 0:512].rearrange("p (k n) -> p k n", k=KT)
        wf1_raw = raw[:, 512:1024].rearrange("p (k n) -> p k n", k=KT)
        wf2_raw = raw[:, 1024:1536].rearrange("p (k n) -> p k n", k=KT)
        wq_raw = raw[:, 1536:1536 + KT * CK].rearrange("p (k n) -> p k n", k=KT)
        wk_raw = raw[:, 1664:1664 + KT * CK].rearrange("p (k n) -> p k n", k=KT)
        id_raw = raw[:, 1792:1920]

        ps_s = ctx.enter_context(nc.psum_tensor("ps_s", [P, 4, W], F32))
        ps_m = ctx.enter_context(nc.psum_tensor("ps_m", [P, 2, W], F32))
        ps_o = ctx.enter_context(nc.psum_tensor("ps_o", [P, KT, W], F32))

        w_loaded, w_loaded2 = sem("w_loaded"), sem("w_loaded2")
        id_zeroed = sem("id_zeroed")
        pick_zeroed = sem("pick_zeroed")
        id_made = sem("id_made")
        w_hi_done = sem("w_hi_done")
        w_split = sem("w_split")
        wvf_ready = sem("wvf_ready")
        wvf_hi_done = sem("wvf_hi_done")
        consts_done = sem("consts_done")
        x_loaded = [sem(f"x_loaded{i}") for i in range(2)]
        x_hi_done = sem("x_hi_done")
        x_split = sem("x_split")
        k_ready, k_hi_done, k_split = sem("k_ready"), sem("k_hi_done"), sem("k_split")
        q_ready, q_hi_done, q_split = sem("q_ready"), sem("q_hi_done"), sem("q_split")
        conv_ready, conv_done = sem("conv_ready"), sem("conv_done")
        v_ready, v_hi_done, v_free = sem("v_ready"), sem("v_hi_done"), sem("v_free")
        q_stat_ready = sem("q_stat_ready")
        m_ready, m_free = sem("m_ready"), sem("m_free")
        neg_max_done, cols_hi_done, cols_ready = sem("neg_max_done"), sem("cols_hi_done"), sem("cols_ready")
        rows_ready, rows_copied, max_rows_copied = sem("rows_ready"), sem("rows_copied"), sem("max_rows_copied")
        s_ready, probs_done, exp_done = sem("s_ready"), sem("probs_done"), sem("exp_done")
        p_hi_done, p_lo_done, pv_done = sem("p_hi_done"), sem("p_lo_done"), sem("pv_done")
        acc_done, acc_folded = sem("acc_done"), sem("acc_folded")
        acc_hi_done, acc_lo_done = sem("acc_hi_done"), sem("acc_lo_done")
        sums0_ready = sem("sums0_ready")
        sums_ready, inv_done, inv_hi_done, inv_cols = sem("sums_ready"), sem("inv_done"), sem("inv_hi_done"), sem("inv_cols")
        o_copied0, o_copied1, o_raw_free = sem("o_copied0"), sem("o_copied1"), sem("o_raw_free")
        factor_ready, o_scaled, finished = sem("factor_ready"), sem("o_scaled"), sem("finished")
        stored = [sem(f"stored{i}") for i in range(CHUNKS)]

        def span(n):
            return bass.ds(n * W, W)

        def snap(eng, value):
            return value if isinstance(value, int) else eng.snap(value)

        def images(eng, project, attend, finish_last):
            def project_image(b, first):
                project(b, 0, 0, not first, False)
                project(b, 0, 1, False, False)
                with eng.Fori(1, CHUNKS // 2 - 1) as c2:
                    project(b, c2, 0, False, False)
                    project(b, c2, 1, False, False)
                project(b, CHUNKS // 2 - 1, 0, False, False)
                project(b, CHUNKS // 2 - 1, 1, False, True)

            def attend_image(b, last_image):
                attend(b, 0, True, False, last_image)
                with eng.Fori(1, LAST) as n:
                    attend(b, n, False, False, last_image)
                attend(b, LAST, False, True, last_image)

            project_image(0, True)
            with eng.Fori(0, IMAGES - 1) as b:
                attend_image(b, False)
                project_image(b + 1, False)
            attend_image(IMAGES - 1, True)
            finish_last(IMAGES * CHUNKS)

        block = ctx.enter_context(nc.Block())

        def load_weights(eng, copies, done):
            for dst, src in copies:
                eng.dma_start(dst, src).then_inc(done, 16)

        @block.sync
        def _(sp):
            load_weights(sp, [
                (wv_raw, wv.rearrange("(k p) n -> p k n", p=P)),
                (wf2_raw, wf2T.rearrange("(k p) n -> p k n", p=P)),
                (bv_c[:], bv), (bf_c[:], bf), (gam[:], gamma.broadcast_to((P, 1))),
                (bq3[0:CK], bq), (bq3[CK:2 * CK], bq), (bq3[2 * CK:R3], bq),
            ], w_loaded)

            def load(b, c):
                sp.dma_start(xf[:, c % 2], x_v[bass.ds(b, 1), :, :, c * W:(c + 1) * W].rearrange(
                    "b p k n -> p (b k) n")).then_inc(x_loaded[c % 2], 16)

            def store(b, n):
                sp.wait_ge(finished, b * CHUNKS + (n + 2))
                sp.dma_start(out_v[bass.ds(b, 1), :, :, n * W:(n + 1) * W].rearrange("b p k n -> p (b k) n"),
                             conv[:, :, n * W:(n + 1) * W]).then_inc(stored[n], 16)

            for c in range(CHUNKS):
                if c >= 2:
                    sp.wait_ge(x_split, c - 1)
                load(0, c)
            with sp.Fori(0, IMAGES - 1) as b:
                stores = {0: (0, 1), 2: range(2, CHUNKS)}
                for c in range(CHUNKS):
                    for n in stores.get(c, ()):
                        store(b, n)
                    sp.wait_ge(x_split, b * CHUNKS + (CHUNKS + c - 1))
                    sp.wait_ge(stored[c], b * 16 + 16)
                    load(b + 1, c)
            for n in range(CHUNKS):
                store(IMAGES - 1, n)
            for n in range(CHUNKS):
                sp.wait_ge(stored[n], 16 * IMAGES)

        @block.tensor
        def _(pe):
            pe.wait_ge(w_loaded, 16 * 8)
            pe.wait_ge(w_loaded2, 16 * 6)
            for ct in range(KT):
                for k in range(KT):
                    nc.tensor.matmul(ps_o[:, ct, 0:C_IN], wv_raw[:, k, ct * P:(ct + 1) * P], wf1_raw[:, k, :],
                                     start=(k == 0), stop=(k == KT - 1))
            for ot in range(KT):
                for k in range(KT):
                    last = nc.tensor.matmul(ps_m[:, ot, 0:1], wf1_raw[:, k, ot * P:(ot + 1) * P], bv_c[:, k:k + 1],
                                            start=(k == 0), stop=(k == KT - 1))
            last.then_inc(wvf_ready, 1)
            pe.wait_ge(w_split, 1)

            def product3(dst, a_hi, a_lo, b_hi, b_lo):
                terms = [(a, b, k) for k in range(KT) for a, b in ((a_hi, b_hi), (a_hi, b_lo), (a_lo, b_hi))]
                for i, (a, b, k) in enumerate(terms):
                    last = nc.tensor.matmul(dst, a(k), b(k), start=(i == 0), stop=(i == len(terms) - 1))
                return last

            def max_scores(B, k):
                i, c = k % QT, k // QT
                pe.wait_ge(m_free, B * MAXMM + k + 1)
                nc.tensor.matmul(ps_m[:, k % 2], q_stat[:, i * P:(i + 1) * P], keys[0:R3, c * W:(c + 1) * W],
                                 start=True, stop=True).then_inc(m_ready, 1)

            def project(b, c2, p, finish_before, last_chunk):
                c = c2 * 2 + p
                C = snap(pe, b * CHUNKS + c)
                xh = lambda k: hi[:, p, k, :]
                xl = lambda k: lo[:, p, k, :]

                def project_keys():
                    product3(ps_s[0:R3, 0], lambda k: wk3_hi[:, k], lambda k: wk3_lo[:, k], xh, xl).then_inc(k_ready, 1)

                def project_queries():
                    product3(ps_s[0:R3, 1], lambda k: wq3_hi[:, k], lambda k: wq3_lo[:, k], xh, xl).then_inc(q_ready, 1)

                def convolve(ot):
                    product3(ps_s[:, 2 + ot], lambda k: wf2_hi[:, k, ot * P:(ot + 1) * P],
                             lambda k: wf2_lo[:, k, ot * P:(ot + 1) * P], xh, xl).then_inc(conv_ready, 1)

                def project_values(j):
                    if j % 2 == 0:
                        pe.wait_ge(v_free, C * 2 + (j // 2 + 1))
                    last = product3(ps_o[:, j // 2, (j % 2) * C_IN:(j % 2 + 1) * C_IN],
                                    lambda k: hi[:, p, k, j * P:(j + 1) * P], lambda k: lo[:, p, k, j * P:(j + 1) * P],
                                    lambda k: wvf_hi[:, k], lambda k: wvf_lo[:, k])
                    if j % 2:
                        last.then_inc(v_ready, 1)

                def max_scores_0(j):
                    if j == 0:
                        pe.wait_ge(k_split, C + 1)
                        pe.wait_ge(q_stat_ready, b * (CHUNKS + 1) + 1)
                    pe.wait_ge(m_free, b * (CHUNKS * MAXMM) + (c * QT + (j + 1)))
                    nc.tensor.matmul(ps_m[:, j % 2], q_stat[:, j * P:(j + 1) * P], keys[0:R3, span(c)],
                                     start=True, stop=True).then_inc(m_ready, 1)

                pe.wait_ge(x_split, C + 1)
                if last_chunk:
                    project_keys()
                    convolve(0)
                    max_scores_0(0)
                    max_scores_0(1)
                    project_queries()
                    max_scores_0(2)
                    max_scores_0(3)
                    convolve(1)
                    project_values(0)
                    turn_columns(b * (CHUNKS + 2) + 1)
                    for j in range(1, JC):
                        project_values(j)
                    pe.wait_ge(max_rows_copied, b * CHUNKS + 1)
                    scores(0, 0)
                    pe.wait_ge(conv_done, C * 2 + 2)
                    scores(0, 1)
                    return
                project_keys()
                if finish_before:
                    sum_probs(b * CHUNKS)
                project_queries()
                if finish_before:
                    turn_columns(b * (CHUNKS + 2))
                convolve(0)
                if finish_before:
                    spread_factor(b * CHUNKS)
                convolve(1)
                if finish_before:
                    pe.wait_ge(o_copied0, b * CHUNKS)
                    pe.wait_ge(o_copied1, b * CHUNKS)
                    pe.wait_ge(o_scaled, b * CHUNKS)
                for j in range(JC):
                    project_values(j)
                    if j == JC - 1:
                        pe.wait_ge(q_split, C + 1)
                        pe.wait_ge(conv_done, C * 2 + 2)
                    max_scores_0(j)

            def turn_columns(B):
                pe.wait_ge(cols_ready, B)
                for i in range(QT):
                    last = nc.tensor.matmul(ps_m[0:RM, 0, i * P:(i + 1) * P], cols[:, i, :], ident[:],
                                            start=True, stop=True)
                last.then_inc(rows_ready, 1)

            def sum_probs(B):
                pe.wait_ge(acc_lo_done, B)
                for i in range(QT):
                    nc.tensor.matmul(ps_m[:, 1, 2 * i:2 * i + 2], acc_hi[:, i * P:(i + 1) * P], ones[:],
                                     start=True, stop=False)
                    last = nc.tensor.matmul(ps_m[:, 1, 2 * i:2 * i + 2], acc_lo[:, i * P:(i + 1) * P], ones[:],
                                            start=False, stop=True)
                last.then_inc(sums_ready, 1)

            def spread_factor(turns):
                pe.wait_ge(rows_copied, turns)
                nc.tensor.matmul(ps_m[:, 1], pick[:], rows[:], start=True, stop=True).then_inc(factor_ready, 1)

            def scores(n, t):
                for h in range(2):
                    j = 2 * t + h
                    last = nc.tensor.matmul(ps_s[:, 2 * (t % 2) + h], keys[:, j * P:(j + 1) * P], queries[:, span(n)],
                                            start=True, stop=True)
                last.then_inc(s_ready, 1)

            def attend(b, n, first, last_block, last_image):
                B = snap(pe, b * CHUNKS + n)
                for t in range(PAIRS):
                    if not first and t == FIN_SLOT:
                        if not last_block:
                            pe.wait_ge(m_free, B * MAXMM + (2 * MAXMM + 2))
                        sum_probs(B)
                    if t == FIN_SLOT + 1:
                        turn_columns(b * (CHUNKS + 2) + (n + 2))
                    if not first and t == FIN_SLOT + 2:
                        spread_factor(B)
                    if not first and t == FIN_SLOT + 3:
                        pe.wait_ge(o_scaled, B)
                    lead = {c: [(v, hi, h, c) for h in range(2) for v in (val_hi, val_lo)] for c in range(KT)}
                    trail = {c: [(val_hi, lo, h, c) for h in range(2)] for c in range(KT)}
                    if t < PAIRS - 1:
                        terms = lead[0] + lead[1] + trail[0] + trail[1]
                    else:
                        terms = lead[0] + trail[0] + lead[1] + trail[1]
                    after_lead = max(i for i, term in enumerate(terms) if term[1] is hi) + 1
                    if t == 0 and not last_block:
                        pe.wait_ge(q_stat_ready, b * (CHUNKS + 1) + (n + 2))
                        max_scores(B + 1, 0)
                        max_scores(B + 1, 1)
                    pe.wait_ge(p_hi_done, B * PAIRS + (t + 1))
                    if t == 0 and first:
                        pe.wait_ge(v_free, b * (2 * CHUNKS) + (2 * CHUNKS + 2))
                    elif t == 0:
                        pe.wait_ge(o_copied0, B)
                    for i, (v, p, h, c) in enumerate(terms):
                        if p is lo and terms[i - 1][1] is hi:
                            pe.wait_ge(p_lo_done, B * PAIRS + (t + 1))
                        if i == after_lead:
                            if t < PAIRS - 2:
                                scores(n, t + 2)
                            elif not last_block:
                                if t == PAIRS - 2:
                                    pe.wait_ge(max_rows_copied, B + 2)
                                scores(n + 1, t + 2 - PAIRS)
                        if t == 0 and i == len(lead[0]) and not first:
                            pe.wait_ge(o_copied1, B)
                        last = nc.tensor.matmul(ps_o[:, c], v[:, 2 * t + h, c * P:(c + 1) * P], p[:, t % 2, h, :],
                                                start=(t == 0 and i in (0, len(lead[0]))),
                                                stop=(t == PAIRS - 1 and i in (5, 11)))
                        if t == PAIRS - 1 and i == 5:
                            last.then_inc(sums0_ready, 1)
                        if i == len(terms) - 1:
                            last.then_inc(pv_done, 1)
                        k = 3 * t + i // 4
                        if not last_block and i % 4 == 1 and k < MAXMM and k > 1:
                            max_scores(B + 1, k)

            def finish_last(B):
                sum_probs(B)
                turn_columns(IMAGES * (CHUNKS + 2))
                spread_factor(B)

            images(pe, project, attend, finish_last)

        @block.scalar
        def _(act):
            load_weights(act, [
                (wk_raw, wkT.rearrange("(k p) n -> p k n", p=P)),
                (wq_raw, wqT.rearrange("(k p) n -> p k n", p=P)),
                (wf1_raw, wf1T.rearrange("(k p) n -> p k n", p=P)),
                (bk3[0:CK], bk), (bk3[CK:2 * CK], bk), (bk3[2 * CK:R3], bk),
            ], w_loaded2)
            act.wait_ge(w_loaded, 16 * 8)
            act.wait_ge(w_loaded2, 16 * 6)
            for r in range(3):
                nc.scalar.activation(wk3_hi[:, :, r * CK:(r + 1) * CK], wk_raw, ACT.Copy)
                nc.scalar.activation(wq3_hi[:, :, r * CK:(r + 1) * CK], wq_raw, ACT.Copy)
            nc.scalar.activation(wf2_hi[:], wf2_raw, ACT.Copy).then_inc(w_hi_done, 1)
            act.wait_ge(wvf_ready, 1)
            nc.scalar.activation(wvf_hi[:], ps_o[:, :, 0:C_IN], ACT.Copy).then_inc(wvf_hi_done, 1)
            act.wait_ge(w_split, 1)

            def split_x(C, p, k, reused):
                act.wait_ge(x_loaded[p], k * 16)
                if reused:
                    act.wait_ge(v_ready, C * 2 - 2)
                nc.scalar.activation(hi[:, p], xf[:, p], ACT.Copy).then_inc(x_hi_done, 1)

            def project(b, c2, p, finish_before, last_chunk):
                c = c2 * 2 + p
                C = snap(act, b * CHUNKS + c)
                if isinstance(C, int) and C == 0:
                    split_x(0, 0, 1, False)
                if finish_before:
                    split_acc(b * CHUNKS)
                act.wait_ge(k_ready, C + 1)
                nc.scalar.activation(keys[0:R3, span(c)], ps_s[0:R3, 0], ACT.Identity, bias=bk3[:, 0:1]).then_inc(k_hi_done, 1)

                def queries_hi():
                    act.wait_ge(q_ready, C + 1)
                    nc.scalar.activation(queries[0:R3, span(c)], ps_s[0:R3, 1], ACT.Identity,
                                         bias=bq3[:, 0:1]).then_inc(q_hi_done, 1)

                def conv_out(ot):
                    act.wait_ge(conv_ready, C * 2 + (ot + 1))
                    nc.scalar.activation(conv[:, ot, span(c)], ps_s[:, 2 + ot], ACT.Identity,
                                         bias=bias[:, ot:ot + 1]).then_inc(conv_done, 1)

                if last_chunk:
                    conv_out(0)
                    queries_hi()
                    conv_out(1)
                else:
                    queries_hi()
                    if finish_before:
                        act.wait_ge(pv_done, b * (CHUNKS * PAIRS))
                    split_x(C + 1, 1 - p, b * (CHUNKS // 2) + (c2 + p) + 1, not (isinstance(c, int) and c == 0))
                    conv_out(0)
                    conv_out(1)
                for h in range(2):
                    act.wait_ge(v_ready, C * 2 + (h + 1))
                    nc.scalar.activation(val_hi[:, bass.ds(c * JC + 2 * h, 2), :],
                                         ps_o[:, h].rearrange("p (j c) -> p j c", j=2), ACT.Copy).then_inc(v_hi_done, 1)
                if last_chunk:
                    exp(b * CHUNKS, 0, None)
                    exp(b * CHUNKS, 1, None)

            def exp(B, t, pool_count):
                banks = ps_s[:, 2 * (t % 2):2 * (t % 2) + 2]
                act.wait_ge(s_ready, B * PAIRS + (t + 1))
                nc.scalar.activation(hi[:, t % 2], banks, ACT.Exp, scale=SCALE).then_inc(p_hi_done, 1)
                if pool_count is not None:
                    act.wait_ge(acc_done, pool_count)
                nc.scalar.activation(probs[:, t % PB], banks, ACT.Exp, scale=SCALE).then_inc(probs_done, 1)
                nc.scalar.activation(banks, banks, ACT.Exp, scale=SCALE).then_inc(exp_done, 1)

            def added(B, t):
                return B * (PAIRS - 1) + max(t, 1)

            def copy_sums(B):
                act.wait_ge(sums0_ready, B)
                act.wait_ge(finished, B)
                nc.scalar.activation(o_raw[:, 0], ps_o[:, 0], ACT.Copy).then_inc(o_copied0, 1)

            def split_acc(B):
                act.wait_ge(acc_folded, B)
                nc.scalar.activation(acc_hi[:], acc_sum[:], ACT.Copy).then_inc(acc_hi_done, 1)

            def attend(b, n, first, last_block, last_image):
                B = snap(act, b * CHUNKS + n)
                for t in range(PAIRS):
                    if t == 2 and not first:
                        split_acc(B)
                    if t == PAIRS - 1:
                        if last_block and not last_image:
                            act.wait_ge(pv_done, B * PAIRS + (PAIRS - 1))
                            split_x(B + 1, 0, b * (CHUNKS // 2) + (CHUNKS // 2 + 1), False)
                        copy_sums(B + 1)
                    ahead = t + 2
                    if ahead < PB:
                        exp(B, ahead, None if first else B * (PAIRS - 1) + (ahead + 1 - PB))
                    elif ahead < PAIRS:
                        exp(B, ahead, added(B, ahead - PB))
                    elif not last_block:
                        exp(B + 1, ahead - PAIRS, added(B, ahead - PB))

            images(act, project, attend, split_acc)

        @block.vector
        def _(dve):
            nc.vector.memset(ones[:].bitcast(F32), 1.0)
            nc.vector.memset(cols[:].bitcast(F32), 0.0)
            nc.vector.memset(keys[R3:RM, :].bitcast(F32), 1.0)
            nc.vector.memset(pick[:].bitcast(F32), 0.0).then_inc(pick_zeroed, 1)
            dve.wait_ge(pick_zeroed, 1)
            nc.vector.memset(pick[0:2].bitcast(F32), 1.0)
            dve.wait_ge(id_made, 1)
            nc.vector.tensor_copy(ident[:], id_raw)
            dve.wait_ge(w_hi_done, 1)
            for r in range(3):
                s = slice(r * CK, (r + 1) * CK)
                nc.vector.tensor_tensor(wk3_lo[:, :, s], wk_raw, wk3_hi[:, :, s].bitcast(F32), ALU.subtract)
                nc.vector.tensor_tensor(wq3_lo[:, :, s], wq_raw, wq3_hi[:, :, s].bitcast(F32), ALU.subtract)
            nc.vector.tensor_tensor(wf2_lo[:], wf2_raw, wf2_hi[:].bitcast(F32), ALU.subtract)
            dve.wait_ge(wvf_hi_done, 1)
            nc.vector.tensor_tensor(wvf_lo[:], ps_o[:, :, 0:C_IN], wvf_hi[:].bitcast(F32), ALU.subtract)
            nc.vector.scalar_tensor_tensor(bias[:], ps_m[:, :, 0], gam[:, 0:1], bf_c[:], ALU.mult, ALU.add).then_inc(w_split, 1)
            dve.sem_inc(v_free, 2)
            dve.sem_inc(m_free, 2)

            def split_x(C, p):
                dve.wait_ge(x_hi_done, C + 1)
                nc.vector.tensor_tensor(lo[:, p], xf[:, p], hi[:, p].bitcast(F32), ALU.subtract).then_inc(x_split, 1)

            def chunk_max(B, i, c):
                dve.wait_ge(m_ready, B * MAXMM + (c * QT + (i + 1)))
                nc.vector.reduce_max(part_max[:, i, bass.ds(c, 1)], ps_m[:, i % 2], AX_X).then_inc(m_free, 1)

            def project(b, c2, p, finish_before, last_chunk):
                c = c2 * 2 + p
                C = snap(dve, b * CHUNKS + c)

                def keys_lo():
                    dve.wait_ge(k_hi_done, C + 1)
                    klo = keys[2 * CK:R3, span(c)]
                    nc.vector.scalar_tensor_tensor(klo, ps_s[2 * CK:R3, 0], bk3[2 * CK:R3, 0:1], klo.bitcast(F32),
                                                   ALU.add, ALU.subtract).then_inc(k_split, 1)

                def queries_lo():
                    dve.wait_ge(q_hi_done, C + 1)
                    qlo = queries[CK:2 * CK, span(c)]
                    nc.vector.scalar_tensor_tensor(qlo, ps_s[CK:2 * CK, 1], bq3[CK:2 * CK, 0:1], qlo.bitcast(F32),
                                                   ALU.add, ALU.subtract).then_inc(q_split, 1)

                def values_lo(h):
                    dve.wait_ge(v_hi_done, C * 2 + (h + 1))
                    split_v(c, h)

                if last_chunk:
                    keys_lo()
                    chunk_max(b * CHUNKS, 0, c)
                    chunk_max(b * CHUNKS, 1, c)
                    queries_lo()
                    chunk_max(b * CHUNKS, 2, c)
                    chunk_max(b * CHUNKS, 3, c)
                    max_columns(b * CHUNKS, True)
                    dve.wait_ge(rows_ready, b * (CHUNKS + 2) + 1)
                    copy_max_rows(0)
                    set_q_stat(1)
                    values_lo(0)
                    values_lo(1)
                    split_p(b * CHUNKS, 0)
                    return
                if isinstance(C, int) and C == 0:
                    split_x(0, 0)
                if finish_before:
                    copy_sums(b * CHUNKS)
                    split_acc(b * CHUNKS)
                keys_lo()
                if finish_before:
                    inv_columns(b * CHUNKS)
                queries_lo()
                if isinstance(c, int) and c == 0:
                    dve.wait_ge(q_split, C + 1)
                    set_q_stat(0)
                if finish_before:
                    dve.wait_ge(rows_ready, b * (CHUNKS + 2))
                    copy_rows()
                split_x(C + 1, 1 - p)
                if finish_before:
                    scale_sums(b * CHUNKS)
                chunk_max(b * CHUNKS, 0, c)
                chunk_max(b * CHUNKS, 1, c)
                values_lo(0)
                chunk_max(b * CHUNKS, 2, c)
                chunk_max(b * CHUNKS, 3, c)
                values_lo(1)

            def split_v(c, h):
                j2 = bass.ds(c * JC + 2 * h, 2)
                nc.vector.tensor_tensor(val_lo[:, j2, :], ps_o[:, h].rearrange("p (j c) -> p j c", j=2),
                                        val_hi[:, j2, :].bitcast(F32), ALU.subtract).then_inc(v_free, 1)

            def split_p(B, t):
                dve.wait_ge(exp_done, B * PAIRS + (t + 1))
                nc.vector.tensor_tensor(lo[:, t % 2], ps_s[:, 2 * (t % 2):2 * (t % 2) + 2],
                                        hi[:, t % 2].bitcast(F32), ALU.subtract).then_inc(p_lo_done, 1)

            def split_acc(B):
                dve.wait_ge(acc_hi_done, B)
                nc.vector.tensor_tensor(acc_lo[:], acc_sum[:], acc_hi[:].bitcast(F32), ALU.subtract).then_inc(acc_lo_done, 1)

            def set_q_stat(n):
                nc.vector.tensor_copy(q_stat[:], queries[0:R3, span(n)].bitcast(F32)).then_inc(q_stat_ready, 1)

            def max_columns(B, turn):
                dve.wait_ge(m_free, B * MAXMM + (MAXMM + 2))
                nc.vector.tensor_reduce(neg_max[:], part_max[:], AX_X, ALU.max, negate=True).then_inc(neg_max_done, 1)
                dve.wait_ge(neg_max_done, B + 1)
                nc.vector.tensor_copy(cols[:, :, R3:R3 + 1], neg_max[:]).then_inc(cols_hi_done, 1)
                dve.wait_ge(cols_hi_done, B + 1)
                last = nc.vector.tensor_tensor(cols[:, :, R3 + 1:R3 + 2], neg_max[:],
                                               cols[:, :, R3:R3 + 1].bitcast(F32), ALU.subtract)
                if turn:
                    last.then_inc(cols_ready, 1)

            def inv_columns(B):
                dve.wait_ge(sums_ready, B)
                nc.vector.reciprocal(inv_sum[:], ps_m[:, 1, 0:2 * QT].rearrange("p (q o) -> p q o", o=2)[:, :, 0:1]).then_inc(inv_done, 1)
                dve.wait_ge(inv_done, B)
                nc.vector.tensor_copy(cols[:, :, 0:1], inv_sum[:]).then_inc(inv_hi_done, 1)
                dve.wait_ge(inv_hi_done, B)
                nc.vector.tensor_tensor(cols[:, :, 1:2], inv_sum[:], cols[:, :, 0:1].bitcast(F32),
                                        ALU.subtract).then_inc(cols_ready, 1)

            def copy_max_rows(n):
                nc.vector.tensor_copy(queries[R3:RM, span(n)], ps_m[R3:RM, 0]).then_inc(max_rows_copied, 1)

            def copy_rows():
                nc.vector.tensor_copy(rows[:], ps_m[0:RM, 0]).then_inc(rows_copied, 1)

            def scale_sums(B):
                dve.wait_ge(o_copied0, B)
                dve.wait_ge(o_copied1, B)
                dve.wait_ge(factor_ready, B)
                nc.vector.scalar_tensor_tensor(o_raw[:], o_raw[:], gam[:, 0:1],
                                               ps_m[:, 1:2, :].broadcast_to((P, KT, W)),
                                               ALU.mult, ALU.mult).then_inc(o_scaled, 1)

            def copy_sums(B):
                dve.wait_ge(pv_done, B * PAIRS)
                dve.wait_ge(finished, B)
                nc.vector.tensor_copy(o_raw[:, 1], ps_o[:, 1]).then_inc(o_copied1, 1)

            def attend(b, n, first, last_block, last_image):
                B = snap(dve, b * CHUNKS + n)
                for t in range(PAIRS):
                    if t == 0 and not first:
                        copy_sums(B)
                    if t == FIN_SLOT:
                        if not last_block:
                            max_columns(B + 1, first)
                        if not first:
                            inv_columns(B)
                    if t == FIN_SLOT + 1:
                        dve.wait_ge(rows_ready, b * (CHUNKS + 2) + (n + 2))
                        if not last_block:
                            copy_max_rows(n + 1)
                        if not first:
                            copy_rows()
                    if t == FIN_SLOT + 2 and not first:
                        scale_sums(B)
                    if t == PAIRS - 1 and not last_block:
                        set_q_stat((n + 2) % CHUNKS)
                    ks = [k for k in (3 * t, 3 * t + 1, 3 * t + 2) if k < MAXMM and not last_block]
                    for k in ks[:2]:
                        chunk_max(B + 1, k % QT, k // QT)
                    if t < PAIRS - 1 or not last_block:
                        if t > 0 or not first:
                            dve.wait_ge(pv_done, B * PAIRS + t)
                        split_p(B, t + 1)
                    for k in ks[2:]:
                        chunk_max(B + 1, k % QT, k // QT)
                    if t == 2 and not first:
                        split_acc(B)
                    if t == PAIRS - 1 and last_block and not last_image:
                        split_x(B + 1, 0)

            def finish_last(B):
                copy_sums(B)
                split_acc(B)
                inv_columns(B)
                dve.wait_ge(rows_ready, IMAGES * (CHUNKS + 2))
                copy_rows()
                scale_sums(B)

            images(dve, project, attend, finish_last)

        @block.gpsimd
        def _(pool):
            nc.gpsimd.memset(id_raw, 0.0).then_inc(id_zeroed, 1)
            pool.wait_ge(id_zeroed, 1)
            nc.gpsimd.affine_select(out=id_raw, in_=id_raw, compare_op=ALU.not_equal, fill=1.0, base=0,
                                    pattern=[[-1, P]], channel_multiplier=1).then_inc(id_made, 1)
            pool.sem_inc(finished, 1)

            def add(B, t):
                pool.wait_ge(probs_done, B * PAIRS + (t + 1))
                if t == 1:
                    nc.gpsimd.tensor_tensor(acc[:], probs[:, 0], probs[:, 1], ALU.add).then_inc(acc_done, 1)
                else:
                    pool.wait_ge(acc_done, B * (PAIRS - 1) + (t - 1))
                    nc.gpsimd.tensor_tensor(acc[:], acc[:], probs[:, t % PB], ALU.add).then_inc(acc_done, 1)

            def finish(B, n):
                pool.wait_ge(o_scaled, B)
                nc.gpsimd.tensor_tensor(conv[:, :, span(n)], conv[:, :, span(n)], o_raw[:], ALU.add).then_inc(finished, 1)

            def project(b, c2, p, finish_before, last_chunk):
                if finish_before:
                    finish(b * CHUNKS, LAST)

            def attend(b, n, first, last_block, last_image):
                B = snap(pool, b * CHUNKS + n)
                if first:
                    add(B, 1)
                for t in range(PAIRS):
                    if t == FIN_SLOT + 2 and not first:
                        finish(B, n - 1)
                    if t == PAIRS - 2:
                        pool.wait_ge(acc_done, B * (PAIRS - 1) + (PAIRS - 1))
                        nc.gpsimd.tensor_tensor(acc_sum[:], acc[:, 0], acc[:, 1], ALU.add).then_inc(acc_folded, 1)
                    if t < PAIRS - 2:
                        add(B, t + 2)
                    elif not last_block and t == PAIRS - 1:
                        pool.wait_ge(acc_folded, B + 1)
                        add(B + 1, 1)

            images(pool, project, attend, lambda B: finish(B, LAST))


def kernel(**inputs):
    import numpy as np
    import concourse.bacc as bacc
    from concourse.bass_utils import run_bass_kernel_spmd

    x = np.asarray(inputs["x"])
    images, c, h, w = x.shape
    wf = np.asarray(inputs["L0_conv_Wf"])
    arrays = {
        "x": x.reshape(images, c, h * w),
        "wqT": np.asarray(inputs["L0_conv_Wq"]).T, "bq": np.asarray(inputs["L0_conv_bq"]).reshape(-1, 1),
        "wkT": np.asarray(inputs["L0_conv_Wk"]).T, "bk": np.asarray(inputs["L0_conv_bk"]).reshape(-1, 1),
        "wv": np.asarray(inputs["L0_conv_Wv"]), "bv": np.asarray(inputs["L0_conv_bv"]).reshape(-1, P).T,
        "gamma": np.asarray(inputs["L0_conv_gamma"]).reshape(1, 1),
        "wf1T": wf[:, :c].T, "wf2T": wf[:, c:].T, "bf": np.asarray(inputs["L0_conv_bf"]).reshape(-1, P).T,
    }
    arrays = {name: np.ascontiguousarray(a) for name, a in arrays.items()}
    nc = bacc.Bacc("TRN2", target_bir_lowering=False, num_devices=1)
    args = [nc.dram_tensor(name, a.shape, mybir.dt.from_np(a.dtype), kind="ExternalInput").ap()
            for name, a in arrays.items()]
    out = nc.dram_tensor("out", (images, c, h * w), F32, kind="ExternalOutput").ap()
    attention_conv(nc, *args, out)
    result = run_bass_kernel_spmd(nc, [arrays], core_ids=[0])
    return result.results[0]["out"].reshape(images, c, h, w)
```

```python
import concourse.bass as bass
from concourse import mybir
from contextlib import ExitStack

F32 = mybir.dt.float32
F32R = mybir.dt.float32r
ALU = mybir.AluOpType
ACT = mybir.ActivationFunctionType
AX_X = mybir.AxisListType.X

P = 128
W = 512


def attention_conv(nc, x, wkqT, wv, wf1T, wf2T, vectors, out):
    IMAGES, C_IN, N = x.shape
    CK = wkqT.shape[1] // 2
    VECTORS = vectors.shape[1]
    KT = C_IN // P
    CHUNKS = N // W
    JT = N // P
    PAIRS = JT // 2
    QT = W // P
    JC = W // P
    MAXMM = QT * CHUNKS
    R3 = 3 * CK
    RM = R3 + 2
    SCALE = float(CK) ** -0.5
    LAST = CHUNKS - 1
    PB = 4
    FIN_SLOT = 11
    IP = 4
    assert C_IN == KT * P == 2 * P and R3 == 96 and CHUNKS == 8 and PAIRS == 16

    x_v = x.rearrange("b (k p) n -> b p k n", p=P)
    out_v = out.rearrange("b (k p) n -> b p k n", p=P)

    with ExitStack() as ctx:
        def sb(name, shape, dt):
            return ctx.enter_context(nc.sbuf_tensor(name, shape, dt))

        def sem(name):
            return ctx.enter_context(nc.semaphore(name))

        keys = sb("keys", [RM, N], F32R)
        queries = sb("queries", [RM, N], F32R)
        q_stat = sb("q_stat", [R3, W], F32R)
        val_hi = sb("val_hi", [P, JT, C_IN], F32R)
        val_lo = sb("val_lo", [P, JT, C_IN], F32R)
        conv = sb("conv", [P, KT, N], F32)
        xf = sb("xf", [P, 2, KT, W], F32)
        probs = sb("probs", [P, PB, 2, W], F32)
        hi = sb("hi", [P, 2, 2, W], F32R)
        lo = sb("lo", [P, 2, 2, W], F32R)
        acc = sb("acc", [P, 2, W], F32)
        acc_sum = sb("acc_sum", [P, W], F32)
        acc_hi = sb("acc_hi", [P, W], F32R)
        acc_lo = sb("acc_lo", [P, W], F32R)
        o_raw = sb("o_raw", [P, KT, W], F32)
        part_max = sb("part_max", [P, QT, CHUNKS], F32)
        cols = sb("cols", [P, QT, RM], F32R)
        inv_sum = sb("inv_sum", [P, W], F32)
        neg_max = sb("neg_max", [P, QT, 1], F32)
        wvf_hi = sb("wvf_hi", [P, KT, C_IN], F32R)
        wvf_lo = sb("wvf_lo", [P, KT, C_IN], F32R)
        wf2_hi = sb("wf2_hi", [P, KT, C_IN], F32R)
        wf2_lo = sb("wf2_lo", [P, KT, C_IN], F32R)
        wkq_hi = sb("wkq_hi", [P, KT, 4, CK], F32R)
        wkq_lo = sb("wkq_lo", [P, KT, 4, CK], F32R)
        kq = sb("kq", [P, W], F32R)
        place_k = sb("place_k", [P, R3], F32R)
        place_q = sb("place_q", [P, R3], F32R)
        ident = sb("ident", [P, P], F32R)
        ones = sb("ones", [P, P], F32R)
        vec = sb("vec", [P, VECTORS], F32)
        bv_c, bf_c, gam = vec[:, 0:KT], vec[:, KT:2 * KT], vec[:, 2 * KT:2 * KT + 1]
        bkq = vec[:, 2 * KT + 1:2 * KT + 2]
        bias = sb("bias", [P, KT], F32)
        raw = conv[:, 0, :]
        wv_raw = raw[:, 0:512].rearrange("p (k n) -> p k n", k=KT)
        wf1_raw = raw[:, 512:1024].rearrange("p (k n) -> p k n", k=KT)
        wf2_raw = raw[:, 1024:1536].rearrange("p (k n) -> p k n", k=KT)
        wkq_raw = raw[:, 1536:1536 + KT * 2 * CK].rearrange("p (k n) -> p k n", k=KT)
        id_raw = raw[:, 1792:1920]

        ps_s = ctx.enter_context(nc.psum_tensor("ps_s", [P, 4, W], F32))
        ps_m = ctx.enter_context(nc.psum_tensor("ps_m", [P, 2, W], F32))
        ps_o = ctx.enter_context(nc.psum_tensor("ps_o", [P, KT, W], F32))

        wkq_loaded, wvf_loaded, wf2_loaded = sem("wkq_loaded"), sem("wvf_loaded"), sem("wf2_loaded")
        vec_loaded = sem("vec_loaded")
        wkq_hi_done, wf2_hi_done, wvf_hi_done = sem("wkq_hi_done"), sem("wf2_hi_done"), sem("wvf_hi_done")
        wkq_split, wf2_split, wvf_split = sem("wkq_split"), sem("wf2_split"), sem("wvf_split")
        wvf_ready = sem("wvf_ready")
        id_zeroed, id_made, key_ones_done = sem("id_zeroed"), sem("id_made"), sem("key_ones_done")
        x_loaded = [sem(f"x_loaded{i}") for i in range(2)]
        x_hi_done, x_split = sem("x_hi_done"), sem("x_split")
        kq_ready, kq_hi_done, kq_split = sem("kq_ready"), sem("kq_hi_done"), sem("kq_split")
        k_placed, q_placed, k_out, q_out = sem("k_placed"), sem("q_placed"), sem("k_out"), sem("q_out")
        conv_ready, conv_done = sem("conv_ready"), sem("conv_done")
        v_ready, v_hi_done, v_free = sem("v_ready"), sem("v_hi_done"), sem("v_free")
        q_stat_ready, m_ready, m_free = sem("q_stat_ready"), sem("m_ready"), sem("m_free")
        neg_max_done, cols_hi_done, cols_ready = sem("neg_max_done"), sem("cols_hi_done"), sem("cols_ready")
        rows_ready, max_rows_copied = sem("rows_ready"), sem("max_rows_copied")
        s_ready, p_hi_done, probs_done, exp_done = sem("s_ready"), sem("p_hi_done"), sem("probs_done"), sem("exp_done")
        p_lo_done, pv_done = sem("p_lo_done"), sem("pv_done")
        acc_done, acc_folded = sem("acc_done"), sem("acc_folded")
        acc_hi_done, acc_lo_done = sem("acc_hi_done"), sem("acc_lo_done")
        sums_ready, last_sums_copied, inv_done = sem("sums_ready"), sem("last_sums_copied"), sem("inv_done")
        sums0_ready, o_copied0, o_copied1 = sem("sums0_ready"), sem("o_copied0"), sem("o_copied1")
        o_scaled, finished = sem("o_scaled"), sem("finished")
        stored = [sem(f"stored{i}") for i in range(CHUNKS)]

        def span(n):
            return bass.ds(n * W, W)

        def snap(eng, value):
            return value if isinstance(value, int) else eng.snap(value)

        def before_last(c):
            return isinstance(c, int) and c == LAST - 1

        def images(eng, project, attend, finish_last):
            def project_image(b, first):
                project(b, 0, 0, None if first else 0, False)
                project(b, 0, 1, None if first else 1, False)
                with eng.Fori(1, CHUNKS // 2 - 1) as c2:
                    project(b, c2, 0, None, False)
                    project(b, c2, 1, None, False)
                project(b, CHUNKS // 2 - 1, 0, None, False)
                project(b, CHUNKS // 2 - 1, 1, None, True)

            def attend_image(b, last_image):
                attend(b, 0, True, False, last_image)
                with eng.Fori(1, LAST) as n:
                    attend(b, n, False, False, last_image)
                attend(b, LAST, False, True, last_image)

            project_image(0, True)
            with eng.Fori(0, IMAGES - 1) as b:
                attend_image(b, False)
                project_image(b + 1, False)
            attend_image(IMAGES - 1, True)
            finish_last(IMAGES * CHUNKS)

        block = ctx.enter_context(nc.Block())

        @block.sync
        def _(sp):
            def load(b, c):
                sp.dma_start(xf[:, c % 2], x_v[bass.ds(b, 1), :, :, c * W:(c + 1) * W].rearrange(
                    "b p k n -> p (b k) n")).then_inc(x_loaded[c % 2], 16)

            def store(b, n):
                sp.wait_ge(finished, b * CHUNKS + (n + 2))
                sp.dma_start(out_v[bass.ds(b, 1), :, :, n * W:(n + 1) * W].rearrange("b p k n -> p (b k) n"),
                             conv[:, :, n * W:(n + 1) * W]).then_inc(stored[n], 16)

            for c in range(CHUNKS):
                if c >= 2:
                    sp.wait_ge(x_split, c - 1)
                load(0, c)
                if c == 0:
                    sp.dma_start(vec[:], vectors).then_inc(vec_loaded, 16)
                    sp.dma_start(wf2_raw, wf2T.rearrange("(k p) n -> p k n", p=P)).then_inc(wf2_loaded, 16)
                    sp.dma_start(wv_raw, wv.rearrange("(k p) n -> p k n", p=P)).then_inc(wvf_loaded, 16)
                    sp.dma_start(wf1_raw, wf1T.rearrange("(k p) n -> p k n", p=P)).then_inc(wvf_loaded, 16)
            with sp.Fori(0, IMAGES - 1) as b:
                stores = {0: (0, 1), 2: range(2, LAST), LAST: (LAST,)}
                for c in range(CHUNKS):
                    for n in stores.get(c, ()):
                        store(b, n)
                    sp.wait_ge(x_split, b * CHUNKS + (CHUNKS + c - 1))
                    sp.wait_ge(stored[c], b * 16 + 16)
                    load(b + 1, c)
            for n in range(CHUNKS):
                store(IMAGES - 1, n)
            for n in range(CHUNKS):
                sp.wait_ge(stored[n], 16 * IMAGES)

        @block.tensor
        def _(pe):
            def fold_weights():
                pe.wait_ge(wvf_loaded, 32)
                pe.wait_ge(vec_loaded, 16)
                for ct in range(KT):
                    for k in range(KT):
                        nc.tensor.matmul(ps_o[:, ct, 0:C_IN], wv_raw[:, k, ct * P:(ct + 1) * P], wf1_raw[:, k, :],
                                         start=(k == 0), stop=(k == KT - 1))
                for ot in range(KT):
                    for k in range(KT):
                        last = nc.tensor.matmul(ps_m[:, ot, 0:1], wf1_raw[:, k, ot * P:(ot + 1) * P], bv_c[:, k:k + 1],
                                                start=(k == 0), stop=(k == KT - 1))
                last.then_inc(wvf_ready, 1)

            def product3(dst, a_hi, a_lo, b_hi, b_lo, halfway=None):
                terms = [(a, b, k) for k in range(KT) for a, b in ((a_hi, b_hi), (a_hi, b_lo), (a_lo, b_hi))]
                for i, (a, b, k) in enumerate(terms):
                    if i == len(terms) // 2 and halfway:
                        halfway()
                    last = nc.tensor.matmul(dst, a(k), b(k), start=(i == 0), stop=(i == len(terms) - 1))
                return last

            def max_scores(B, k):
                i, c = k % QT, k // QT
                pe.wait_ge(m_free, B * MAXMM + k + 1)
                nc.tensor.matmul(ps_m[:, k % 2], q_stat[:, i * P:(i + 1) * P], keys[0:R3, c * W:(c + 1) * W],
                                 start=True, stop=True).then_inc(m_ready, 1)

            def project(b, c2, p, finishing, last_chunk):
                c = c2 * 2 + p
                C = snap(pe, b * CHUNKS + c)
                def project_kq(p):
                    product3(ps_s[:, 0], lambda k: wkq_hi[:, k], lambda k: wkq_lo[:, k],
                             lambda k: hi[:, p, k, :], lambda k: lo[:, p, k, :]).then_inc(kq_ready, 1)

                def place_kq():
                    pe.wait_ge(kq_split, C + 1)
                    nc.tensor.matmul(ps_s[0:R3, 0], place_k[:], kq[:], start=True, stop=True).then_inc(k_placed, 1)
                    nc.tensor.matmul(ps_s[0:R3, 1], place_q[:], kq[:], start=True, stop=True).then_inc(q_placed, 1)

                def convolve(ot, halfway=None):
                    product3(ps_s[:, 2 + ot], lambda k: wf2_hi[:, k, ot * P:(ot + 1) * P],
                             lambda k: wf2_lo[:, k, ot * P:(ot + 1) * P],
                             lambda k: hi[:, p, k, :], lambda k: lo[:, p, k, :], halfway).then_inc(conv_ready, 1)

                def project_values(j):
                    if j % 2 == 0:
                        pe.wait_ge(v_free, C * 2 + (j // 2 + 1))
                    last = product3(ps_o[:, j // 2, (j % 2) * C_IN:(j % 2 + 1) * C_IN],
                                    lambda k: hi[:, p, k, j * P:(j + 1) * P], lambda k: lo[:, p, k, j * P:(j + 1) * P],
                                    lambda k: wvf_hi[:, k], lambda k: wvf_lo[:, k])
                    if j % 2:
                        last.then_inc(v_ready, 1)

                def max_scores_0(j):
                    if j == 0:
                        pe.wait_ge(k_out, C + 1)
                        pe.wait_ge(q_stat_ready, b * (CHUNKS + 1) + 1)
                    pe.wait_ge(m_free, b * (CHUNKS * MAXMM) + (c * QT + (j + 1)))
                    nc.tensor.matmul(ps_m[:, j % 2], q_stat[:, j * P:(j + 1) * P], keys[0:R3, span(c)],
                                     start=True, stop=True).then_inc(m_ready, 1)

                pe.wait_ge(x_split, C + 1)
                if last_chunk:
                    place_kq()
                    convolve(0, lambda: (max_scores_0(0), max_scores_0(1)))
                    convolve(1, lambda: (max_scores_0(2), max_scores_0(3)))
                    project_values(0)
                    project_values(1)
                    turn_columns(b * CHUNKS)
                    project_values(2)
                    project_values(3)
                    pe.wait_ge(q_out, C + 1)
                    pe.wait_ge(max_rows_copied, b * CHUNKS + 1)
                    scores(0, 0)
                    pe.wait_ge(conv_done, C * 2 + 2)
                    scores(0, 1)
                    return
                very_first = isinstance(C, int) and C == 0
                if very_first:
                    pe.wait_ge(wkq_split, 1)
                project_kq(p)
                if very_first:
                    fold_weights()
                    pe.wait_ge(wf2_split, 1)
                convolve(0)
                if finishing == 0:
                    sum_probs(b * CHUNKS)
                convolve(1, place_kq)
                if very_first:
                    pe.wait_ge(wvf_split, 1)
                    pe.wait_ge(key_ones_done, 1)
                if finishing == 0:
                    pe.wait_ge(o_copied0, b * CHUNKS)
                    pe.wait_ge(o_copied1, b * CHUNKS)
                for j in range(JC):
                    if j == JC // 2 and before_last(c):
                        pe.wait_ge(x_split, C + 2)
                        project_kq(1 - p)
                    project_values(j)
                    if j == JC - 1:
                        pe.wait_ge(q_out, C + 1)
                        pe.wait_ge(conv_done, C * 2 + 2)
                    if j == 1 and finishing == 0:
                        pe.wait_ge(last_sums_copied, b)
                    max_scores_0(j)

            def turn_columns(B):
                pe.wait_ge(cols_ready, B + 1)
                for i in range(QT):
                    last = nc.tensor.matmul(ps_m[0:RM, 0, i * P:(i + 1) * P], cols[:, i, :], ident[:],
                                            start=True, stop=True)
                last.then_inc(rows_ready, 1)

            def sum_probs(B):
                pe.wait_ge(acc_lo_done, B)
                nc.tensor.matmul(ps_m[:, 1], ones[:], acc_hi[:], start=True, stop=False)
                nc.tensor.matmul(ps_m[:, 1], ones[:], acc_lo[:], start=False, stop=True).then_inc(sums_ready, 1)

            def scores(n, t):
                for h in range(2):
                    j = 2 * t + h
                    last = nc.tensor.matmul(ps_s[:, 2 * (t % 2) + h], keys[:, j * P:(j + 1) * P], queries[:, span(n)],
                                            start=True, stop=True)
                last.then_inc(s_ready, 1)

            def attend(b, n, first, last_block, last_image):
                B = snap(pe, b * CHUNKS + n)
                for t in range(PAIRS):
                    if not first and t == FIN_SLOT:
                        if not last_block:
                            pe.wait_ge(m_free, B * MAXMM + (2 * MAXMM + 2))
                        sum_probs(B)
                    if t == FIN_SLOT + 1 and not last_block:
                        turn_columns(B + 1)
                    if not first and t == FIN_SLOT + 4:
                        pe.wait_ge(inv_done, B * IP)
                    lead = {c: [(v, hi, h, c) for h in range(2) for v in (val_hi, val_lo)] for c in range(KT)}
                    trail = {c: [(val_hi, lo, h, c) for h in range(2)] for c in range(KT)}
                    if t < PAIRS - 1:
                        terms = lead[0] + lead[1] + trail[0] + trail[1]
                    else:
                        terms = lead[0] + trail[0] + lead[1] + trail[1]
                    after_lead = max(i for i, term in enumerate(terms) if term[1] is hi) + 1
                    if t == 0 and not last_block:
                        pe.wait_ge(q_stat_ready, b * (CHUNKS + 1) + (n + 2))
                        max_scores(B + 1, 0)
                        max_scores(B + 1, 1)
                    pe.wait_ge(p_hi_done, B * PAIRS + (t + 1))
                    if t == 0 and first:
                        pe.wait_ge(v_free, b * (2 * CHUNKS) + (2 * CHUNKS + 2))
                    elif t == 0:
                        pe.wait_ge(o_copied0, B)
                    for i, (v, p, h, c) in enumerate(terms):
                        if p is lo and terms[i - 1][1] is hi:
                            pe.wait_ge(p_lo_done, B * PAIRS + (t + 1))
                        if i == after_lead:
                            if t < PAIRS - 2:
                                scores(n, t + 2)
                            elif not last_block:
                                if t == PAIRS - 2:
                                    pe.wait_ge(max_rows_copied, B + 2)
                                scores(n + 1, t + 2 - PAIRS)
                        if t == 0 and i == len(lead[0]) and not first:
                            pe.wait_ge(o_copied1, B)
                        last = nc.tensor.matmul(ps_o[:, c], v[:, 2 * t + h, c * P:(c + 1) * P], p[:, t % 2, h, :],
                                                start=(t == 0 and i in (0, len(lead[0]))),
                                                stop=(t == PAIRS - 1 and i in (5, 11)))
                        if t == PAIRS - 1 and i == 5:
                            last.then_inc(sums0_ready, 1)
                        if i == len(terms) - 1:
                            last.then_inc(pv_done, 1)
                        k = 3 * t + i // 4
                        if not last_block and i % 4 == 1 and k < MAXMM and k > 1:
                            max_scores(B + 1, k)

            def finish_last(B):
                sum_probs(B)

            images(pe, project, attend, finish_last)

        @block.scalar
        def _(act):
            act.dma_start(wkq_raw, wkqT.rearrange("(k p) n -> p k n", p=P)).then_inc(wkq_loaded, 16)
            act.wait_ge(id_made, 1)
            nc.scalar.activation(inv_sum[:, 0:1], id_raw[:, 0:1], ACT.Exp)
            act.wait_ge(wkq_loaded, 16)
            nc.scalar.activation(wkq_hi[:].rearrange("p k (r u) c -> p k r (u c)", r=2),
                                 wkq_raw.unsqueeze(2).broadcast_to((P, KT, 2, 2 * CK)), ACT.Copy).then_inc(wkq_hi_done, 1)

            def split_x(C, p, k, reused):
                act.wait_ge(x_loaded[p], k * 16)
                if reused:
                    act.wait_ge(v_ready, C * 2 - 2)
                nc.scalar.activation(hi[:, p], xf[:, p], ACT.Copy).then_inc(x_hi_done, 1)

            def kq_hi(C):
                act.wait_ge(kq_ready, C + 1)
                nc.scalar.activation(kq[:], ps_s[:, 0], ACT.Identity, bias=bkq).then_inc(kq_hi_done, 1)

            def project(b, c2, p, finishing, last_chunk):
                c = c2 * 2 + p
                C = snap(act, b * CHUNKS + c)
                if isinstance(C, int) and C == 0:
                    split_x(0, 0, 1, False)
                    act.wait_ge(wf2_loaded, 16)
                    nc.scalar.activation(wf2_hi[:], wf2_raw, ACT.Copy).then_inc(wf2_hi_done, 1)
                if finishing == 0:
                    split_acc(b * CHUNKS)
                if isinstance(C, int) and C == 0:
                    act.wait_ge(vec_loaded, 16)
                if not last_chunk:
                    kq_hi(C)
                if isinstance(C, int) and C == 0:
                    act.wait_ge(wvf_ready, 1)
                    nc.scalar.activation(wvf_hi[:], ps_o[:, :, 0:C_IN], ACT.Copy).then_inc(wvf_hi_done, 1)
                    act.wait_ge(wvf_split, 1)

                def keys_out():
                    act.wait_ge(k_placed, C + 1)
                    nc.scalar.activation(keys[0:R3, span(c)], ps_s[0:R3, 0], ACT.Copy).then_inc(k_out, 1)

                def queries_out():
                    act.wait_ge(q_placed, C + 1)
                    nc.scalar.activation(queries[0:R3, span(c)], ps_s[0:R3, 1], ACT.Copy).then_inc(q_out, 1)

                def conv_out(ot):
                    act.wait_ge(conv_ready, C * 2 + (ot + 1))
                    nc.scalar.activation(conv[:, ot, span(c)], ps_s[:, 2 + ot], ACT.Identity,
                                         bias=bias[:, ot:ot + 1]).then_inc(conv_done, 1)

                if finishing == 0:
                    act.wait_ge(sums_ready, b * CHUNKS)
                    nc.scalar.activation(inv_sum[:], ps_m[:, 1], ACT.Copy).then_inc(last_sums_copied, 1)
                if finishing == 0 or last_chunk:
                    keys_out()
                    queries_out()
                if finishing == 0:
                    act.wait_ge(pv_done, b * (CHUNKS * PAIRS))
                if not last_chunk:
                    split_x(C + 1, 1 - p, b * (CHUNKS // 2) + (c2 + p) + 1, not (isinstance(c, int) and c == 0))
                conv_out(0)
                if finishing != 0 and not last_chunk:
                    keys_out()
                    queries_out()
                conv_out(1)
                for h in range(2):
                    act.wait_ge(v_ready, C * 2 + (h + 1))
                    nc.scalar.activation(val_hi[:, bass.ds(c * JC + 2 * h, 2), :],
                                         ps_o[:, h].rearrange("p (j c) -> p j c", j=2), ACT.Copy).then_inc(v_hi_done, 1)
                    if h == 0 and before_last(c):
                        kq_hi(C + 1)
                if last_chunk:
                    B = b * CHUNKS
                    act.wait_ge(s_ready, B * PAIRS + 1)
                    nc.scalar.activation(hi[:, 0], ps_s[:, 0:2], ACT.Exp, scale=SCALE).then_inc(p_hi_done, 1)
                    nc.scalar.activation(probs[:, 0], ps_s[:, 0:2], ACT.Exp, scale=SCALE).then_inc(probs_done, 1)
                    act.sem_inc(exp_done, 1)
                    exp(b * CHUNKS, 1, None)

            def exp(B, t, pool_count):
                banks = ps_s[:, 2 * (t % 2):2 * (t % 2) + 2]
                act.wait_ge(s_ready, B * PAIRS + (t + 1))
                nc.scalar.activation(hi[:, t % 2], banks, ACT.Exp, scale=SCALE).then_inc(p_hi_done, 1)
                if pool_count is not None:
                    act.wait_ge(acc_done, pool_count)
                nc.scalar.activation(probs[:, t % PB], banks, ACT.Exp, scale=SCALE).then_inc(probs_done, 1)
                nc.scalar.activation(banks, banks, ACT.Exp, scale=SCALE).then_inc(exp_done, 1)

            def added(B, t):
                return B * (PAIRS - 1) + max(t, 1)

            def copy_sums(B):
                act.wait_ge(sums0_ready, B)
                act.wait_ge(finished, B)
                nc.scalar.activation(o_raw[:, 0], ps_o[:, 0], ACT.Identity, scale=gam).then_inc(o_copied0, 1)

            def split_acc(B):
                act.wait_ge(acc_folded, B)
                nc.scalar.activation(acc_hi[:], acc_sum[:], ACT.Copy).then_inc(acc_hi_done, 1)

            def attend(b, n, first, last_block, last_image):
                B = snap(act, b * CHUNKS + n)
                for t in range(PAIRS):
                    if t == 2 and not first:
                        split_acc(B)
                    if t == PAIRS - 1:
                        if last_block and not last_image:
                            act.wait_ge(pv_done, B * PAIRS + (PAIRS - 1))
                            split_x(B + 1, 0, b * (CHUNKS // 2) + (CHUNKS // 2 + 1), False)
                        copy_sums(B + 1)
                    ahead = t + 2
                    if ahead < PB:
                        exp(B, ahead, None if first else B * (PAIRS - 1) + (ahead + 1 - PB))
                    elif ahead < PAIRS:
                        exp(B, ahead, added(B, ahead - PB))
                    elif not last_block:
                        exp(B + 1, ahead - PAIRS, added(B, ahead - PB))

            images(act, project, attend, split_acc)

        @block.vector
        def _(dve):
            nc.vector.memset(ones[:].bitcast(F32), 1.0)
            nc.vector.memset(cols[:].bitcast(F32), 0.0)
            dve.wait_ge(wkq_hi_done, 1)
            nc.vector.tensor_tensor(wkq_lo[:].rearrange("p k (r u) c -> p k r (u c)", r=2),
                                    wkq_raw.unsqueeze(2).broadcast_to((P, KT, 2, 2 * CK)),
                                    wkq_hi[:].bitcast(F32).rearrange("p k (r u) c -> p k r (u c)", r=2),
                                    ALU.subtract).then_inc(wkq_split, 1)

            def setup_constants():
                dve.wait_ge(id_made, 1)
                nc.vector.tensor_copy(ident[:], id_raw)
                for g, (from_k, from_q) in enumerate([(0, 1), (0, 3), (2, 1)]):
                    s = slice(g * CK, (g + 1) * CK)
                    nc.vector.tensor_copy(place_k[:, s], id_raw[:, from_k * CK:(from_k + 1) * CK])
                    nc.vector.tensor_copy(place_q[:, s], id_raw[:, from_q * CK:(from_q + 1) * CK])

            def setup_wf2():
                dve.wait_ge(wf2_hi_done, 1)
                nc.vector.tensor_tensor(wf2_lo[:], wf2_raw, wf2_hi[:].bitcast(F32), ALU.subtract).then_inc(wf2_split, 1)

            def setup_values():
                dve.wait_ge(wvf_hi_done, 1)
                nc.vector.tensor_tensor(wvf_lo[:], ps_o[:, :, 0:C_IN], wvf_hi[:].bitcast(F32), ALU.subtract)
                nc.vector.scalar_tensor_tensor(bias[:], ps_m[:, :, 0], gam, bf_c, ALU.mult, ALU.add).then_inc(wvf_split, 1)

            dve.sem_inc(v_free, 2)
            dve.sem_inc(m_free, 2)

            def split_x(C, p):
                dve.wait_ge(x_hi_done, C + 1)
                nc.vector.tensor_tensor(lo[:, p], xf[:, p], hi[:, p].bitcast(F32), ALU.subtract).then_inc(x_split, 1)

            def chunk_max(B, i, c):
                dve.wait_ge(m_ready, B * MAXMM + (c * QT + (i + 1)))
                nc.vector.reduce_max(part_max[:, i, bass.ds(c, 1)], ps_m[:, i % 2], AX_X).then_inc(m_free, 1)

            def project(b, c2, p, finishing, last_chunk):
                c = c2 * 2 + p
                C = snap(dve, b * CHUNKS + c)

                def kq_lo(C):
                    dve.wait_ge(kq_hi_done, C + 1)
                    tail = kq[2 * CK:4 * CK]
                    nc.vector.scalar_tensor_tensor(tail, ps_s[2 * CK:4 * CK, 0], bkq[2 * CK:4 * CK], tail.bitcast(F32),
                                                   ALU.add, ALU.subtract).then_inc(kq_split, 1)

                def values_lo(h):
                    dve.wait_ge(v_hi_done, C * 2 + (h + 1))
                    split_v(c, h)

                if last_chunk:
                    chunk_max(b * CHUNKS, 0, c)
                    chunk_max(b * CHUNKS, 1, c)
                    chunk_max(b * CHUNKS, 2, c)
                    chunk_max(b * CHUNKS, 3, c)
                    max_columns(b * CHUNKS)
                    copy_max_rows(b * CHUNKS, 0)
                    set_q_stat(1)
                    values_lo(0)
                    values_lo(1)
                    dve.wait_ge(probs_done, b * CHUNKS * PAIRS + 1)
                    nc.vector.tensor_tensor(lo[:, 0], probs[:, 0], hi[:, 0].bitcast(F32), ALU.subtract).then_inc(p_lo_done, 1)
                    return
                if isinstance(C, int) and C == 0:
                    split_x(0, 0)
                    setup_wf2()
                    setup_constants()
                if finishing == 0:
                    copy_sums(b * CHUNKS)
                    split_acc(b * CHUNKS)
                kq_lo(C)
                if isinstance(C, int) and C == 0:
                    setup_values()
                if finishing == 0:
                    invert_copied_sums(b, (0, 1))
                if isinstance(c, int) and c == 0:
                    dve.wait_ge(q_out, C + 1)
                    set_q_stat(0)
                if finishing == 0:
                    chunk_max(b * CHUNKS, 0, c)
                    split_x(C + 1, 1 - p)
                else:
                    split_x(C + 1, 1 - p)
                    if finishing == 1:
                        invert_copied_sums(b, (2, 3))
                    chunk_max(b * CHUNKS, 0, c)
                chunk_max(b * CHUNKS, 1, c)
                values_lo(0)
                if before_last(c):
                    kq_lo(C + 1)
                chunk_max(b * CHUNKS, 2, c)
                chunk_max(b * CHUNKS, 3, c)
                values_lo(1)

            def split_v(c, h):
                j2 = bass.ds(c * JC + 2 * h, 2)
                nc.vector.tensor_tensor(val_lo[:, j2, :], ps_o[:, h].rearrange("p (j c) -> p j c", j=2),
                                        val_hi[:, j2, :].bitcast(F32), ALU.subtract).then_inc(v_free, 1)

            def split_p(B, t):
                dve.wait_ge(exp_done, B * PAIRS + (t + 1))
                nc.vector.tensor_tensor(lo[:, t % 2], ps_s[:, 2 * (t % 2):2 * (t % 2) + 2],
                                        hi[:, t % 2].bitcast(F32), ALU.subtract).then_inc(p_lo_done, 1)

            def split_acc(B):
                dve.wait_ge(acc_hi_done, B)
                nc.vector.tensor_tensor(acc_lo[:], acc_sum[:], acc_hi[:].bitcast(F32), ALU.subtract).then_inc(acc_lo_done, 1)

            def set_q_stat(n):
                nc.vector.tensor_copy(q_stat[:], queries[0:R3, span(n)].bitcast(F32)).then_inc(q_stat_ready, 1)

            def max_columns(B):
                dve.wait_ge(m_free, B * MAXMM + (MAXMM + 2))
                nc.vector.tensor_reduce(neg_max[:], part_max[:], AX_X, ALU.max, negate=True).then_inc(neg_max_done, 1)
                dve.wait_ge(neg_max_done, B + 1)
                nc.vector.tensor_copy(cols[:, :, R3:R3 + 1], neg_max[:]).then_inc(cols_hi_done, 1)
                dve.wait_ge(cols_hi_done, B + 1)
                nc.vector.tensor_tensor(cols[:, :, R3 + 1:R3 + 2], neg_max[:], cols[:, :, R3:R3 + 1].bitcast(F32),
                                        ALU.subtract).then_inc(cols_ready, 1)

            def invert_copied_sums(b, parts):
                dve.wait_ge(last_sums_copied, b)
                for i in parts:
                    s = slice(i * (W // IP), (i + 1) * (W // IP))
                    nc.vector.reciprocal(inv_sum[:, s], inv_sum[:, s]).then_inc(inv_done, 1)

            def invert_sums(B, parts):
                dve.wait_ge(sums_ready, B)
                for i in parts:
                    s = slice(i * (W // IP), (i + 1) * (W // IP))
                    nc.vector.reciprocal(inv_sum[:, s], ps_m[:, 1, s]).then_inc(inv_done, 1)

            def copy_max_rows(B, n):
                dve.wait_ge(rows_ready, B + 1)
                nc.vector.tensor_copy(queries[R3:RM, span(n)], ps_m[R3:RM, 0]).then_inc(max_rows_copied, 1)

            def scale_sums(B):
                dve.wait_ge(o_copied0, B)
                dve.wait_ge(o_copied1, B)
                dve.wait_ge(inv_done, B * IP)
                nc.vector.tensor_tensor(o_raw[:], o_raw[:], inv_sum[:].unsqueeze(1).broadcast_to((P, KT, W)),
                                        ALU.mult).then_inc(o_scaled, 1)

            def copy_sums(B):
                dve.wait_ge(pv_done, B * PAIRS)
                dve.wait_ge(finished, B)
                nc.vector.tensor_scalar(o_raw[:, 1], ps_o[:, 1], gam, None, ALU.mult).then_inc(o_copied1, 1)

            def attend(b, n, first, last_block, last_image):
                B = snap(dve, b * CHUNKS + n)
                for t in range(PAIRS):
                    if t == 0 and not first:
                        copy_sums(B)
                    if t == FIN_SLOT and not last_block:
                        max_columns(B + 1)
                    if t == FIN_SLOT and not first:
                        invert_sums(B, range(0, 2))
                    if t == FIN_SLOT + 1 and not last_block:
                        copy_max_rows(B + 1, n + 1)
                    if t == FIN_SLOT + 1 and not first:
                        invert_sums(B, range(2, 3))
                    if t == FIN_SLOT + 2 and not first:
                        invert_sums(B, range(3, 4))
                        scale_sums(B)
                    if t == PAIRS - 1 and not last_block:
                        set_q_stat((n + 2) % CHUNKS)
                    ks = [k for k in (3 * t, 3 * t + 1, 3 * t + 2) if k < MAXMM and not last_block]
                    for k in ks[:2]:
                        chunk_max(B + 1, k % QT, k // QT)
                    if t < PAIRS - 1 or not last_block:
                        if t > 0 or not first:
                            dve.wait_ge(pv_done, B * PAIRS + t)
                        split_p(B, t + 1)
                    for k in ks[2:]:
                        chunk_max(B + 1, k % QT, k // QT)
                    if t == 2 and not first:
                        split_acc(B)
                    if t == PAIRS - 1 and last_block and not last_image:
                        split_x(B + 1, 0)

            def finish_last(B):
                copy_sums(B)
                split_acc(B)
                invert_sums(B, range(IP))
                scale_sums(B)
                dve.wait_ge(o_scaled, B)
                dve.wait_ge(finished, B)
                nc.vector.tensor_tensor(conv[:, :, span(LAST)], conv[:, :, span(LAST)], o_raw[:],
                                        ALU.add).then_inc(finished, 1)

            images(dve, project, attend, finish_last)

        @block.gpsimd
        def _(pool):
            nc.gpsimd.memset(id_raw, 0.0).then_inc(id_zeroed, 1)
            pool.wait_ge(id_zeroed, 1)
            nc.gpsimd.affine_select(out=id_raw, in_=id_raw, compare_op=ALU.not_equal, fill=1.0, base=0,
                                    pattern=[[-1, P]], channel_multiplier=1).then_inc(id_made, 1)
            pool.wait_ge(id_made, 1)
            nc.gpsimd.memset(keys[R3:RM, :].bitcast(F32), 1.0).then_inc(key_ones_done, 1)
            pool.sem_inc(finished, 1)

            def add(B, t):
                pool.wait_ge(probs_done, B * PAIRS + (t + 1))
                if t == 1:
                    nc.gpsimd.tensor_tensor(acc[:], probs[:, 0], probs[:, 1], ALU.add).then_inc(acc_done, 1)
                else:
                    pool.wait_ge(acc_done, B * (PAIRS - 1) + (t - 1))
                    nc.gpsimd.tensor_tensor(acc[:], acc[:], probs[:, t % PB], ALU.add).then_inc(acc_done, 1)

            def finish(B, n):
                pool.wait_ge(o_scaled, B)
                nc.gpsimd.tensor_tensor(conv[:, :, span(n)], conv[:, :, span(n)], o_raw[:], ALU.add).then_inc(finished, 1)

            def project(b, c2, p, finishing, last_chunk):
                if finishing == 0:
                    B = b * CHUNKS
                    pool.wait_ge(o_copied0, B)
                    pool.wait_ge(o_copied1, B)
                    pool.wait_ge(inv_done, B * IP)
                    nc.gpsimd.tensor_tensor(o_raw[:], o_raw[:], inv_sum[:].unsqueeze(1).broadcast_to((P, KT, W)),
                                            ALU.mult).then_inc(o_scaled, 1)
                    finish(B, LAST)

            def attend(b, n, first, last_block, last_image):
                B = snap(pool, b * CHUNKS + n)
                if first:
                    add(B, 1)
                for t in range(PAIRS):
                    if t == FIN_SLOT + 2 and not first:
                        finish(B, n - 1)
                    if t == PAIRS - 2:
                        pool.wait_ge(acc_done, B * (PAIRS - 1) + (PAIRS - 1))
                        nc.gpsimd.tensor_tensor(acc_sum[:], acc[:, 0], acc[:, 1], ALU.add).then_inc(acc_folded, 1)
                    if t < PAIRS - 2:
                        add(B, t + 2)
                    elif not last_block and t == PAIRS - 1:
                        pool.wait_ge(acc_folded, B + 1)
                        add(B + 1, 1)

            images(pool, project, attend, lambda B: None)


def kernel(**inputs):
    import numpy as np
    import concourse.bacc as bacc
    from concourse.bass_utils import run_bass_kernel_spmd

    x = np.asarray(inputs["x"])
    images, c, h, w = x.shape
    arg = {name.removeprefix("L0_conv_"): np.asarray(a) for name, a in inputs.items()}
    vectors = np.zeros((P, 2 * (c // P) + 2), np.float32)
    vectors[:, 0:c // P] = arg["bv"].reshape(-1, P).T
    vectors[:, c // P:2 * (c // P)] = arg["bf"].reshape(-1, P).T
    vectors[:, -2] = arg["gamma"]
    vectors[:, -1] = np.concatenate([arg["bk"], arg["bq"], arg["bk"], arg["bq"]])
    arrays = {
        "x": x.reshape(images, c, h * w),
        "wkqT": np.concatenate([arg["Wk"], arg["Wq"]]).T,
        "wv": arg["Wv"],
        "wf1T": arg["Wf"][:, :c].T, "wf2T": arg["Wf"][:, c:].T,
        "vectors": vectors,
    }
    arrays = {name: np.ascontiguousarray(a) for name, a in arrays.items()}
    nc = bacc.Bacc("TRN2", target_bir_lowering=False, num_devices=1)
    args = [nc.dram_tensor(name, a.shape, mybir.dt.from_np(a.dtype), kind="ExternalInput").ap()
            for name, a in arrays.items()]
    out = nc.dram_tensor("out", (images, c, h * w), F32, kind="ExternalOutput").ap()
    attention_conv(nc, *args, out)
    result = run_bass_kernel_spmd(nc, [arrays], core_ids=[0])
    return result.results[0]["out"].reshape(images, c, h, w)
```
